# Optimizing a Trainium2 kernel written in Bass

```python
import numpy as np
import jax
import jax.numpy as jnp

def _softmax(x, axis=-1):
    return jax.nn.softmax(x, axis=axis)

def _gelu(x):
    return jax.nn.gelu(x, approximate=True)

def _silu(x):
    return jax.nn.silu(x)

def _sigmoid(x):
    return jax.nn.sigmoid(x)

def _layernorm(x, axis=-1, eps=1e-05):
    m = jnp.mean(x, axis=axis, keepdims=True)
    v = jnp.var(x, axis=axis, keepdims=True)
    return (x - m) / jnp.sqrt(v + eps)

def _scatter_add(tgt, idx, src, axis=0):
    return tgt.at[idx].add(src)

def _segment_sum(src, seg, n):
    return jax.ops.segment_sum(src, seg, n)
kernel_name = 'mk_cond_resid_d2_seqx_r2_8d4c5d'

def setup_inputs(seed: int=0):
    np.random.seed(seed)
    _w = jnp.asarray

    def _rec_inputs():
        import jax
        import jax.numpy as jnp
        _rk = jax.random.key(seed)
        x = 7.22e-05 + 1 * jax.random.normal(jax.random.fold_in(_rk, 1), (8, 1024, 512), jnp.float32)
        _lenS = 1024 - jax.random.randint(jax.random.fold_in(_rk, 7), (8,), 0, max(1, 1024 // 4) + 1, jnp.int32)
        _lenS2 = 1024 - jax.random.randint(jax.random.fold_in(_rk, 8), (8,), 0, max(1, 1024 // 4) + 1, jnp.int32)
        itok_BxS_0_999 = jax.random.randint(jax.random.fold_in(_rk, 11), (8, 1024), 0, 500, jnp.int32)
        itok_BxS_0_4 = jax.random.randint(jax.random.fold_in(_rk, 12), (8, 1024), 0, 5, jnp.int32)
        cond_512 = 0.00199304 + 1.00034 * jax.random.normal(jax.random.fold_in(_rk, 14), (8, 256), jnp.float32)
        cond_64 = 0.0990542 + 1.04422 * jax.random.normal(jax.random.fold_in(_rk, 15), (8, 64), jnp.float32)
        fside_Bx32_0 = -0.136436 + 0.990155 * jax.random.normal(jax.random.fold_in(_rk, 16), (8, 32), jnp.float32)
        _validS = jnp.arange(1024)[None, :] < _lenS[:, None]
        _validS2 = jnp.arange(1024)[None, :] < _lenS2[:, None]
        _causal = jnp.tril(jnp.ones((1024, 1024), dtype=bool))
        mask_BxS_ik0 = jnp.where(jnp.broadcast_to(_validS[:, :], (8, 1024)), 0, 1).astype(jnp.int32)
        return (x, itok_BxS_0_999, itok_BxS_0_4, cond_512, cond_64, fside_Bx32_0, mask_BxS_ik0)
    x, itok_BxS_0_999, itok_BxS_0_4, cond_512, cond_64, fside_Bx32_0, mask_BxS_ik0 = _rec_inputs()

    def _L0_cond_setup():
        import jax, jax.numpy as jnp
        import numpy as np
        EPS = 1e-05

        def _ln(x, g, b):
            m = jnp.mean(x, axis=-1, keepdims=True)
            v = jnp.mean((x - m) ** 2, axis=-1, keepdims=True)
            return (x - m) * jax.lax.rsqrt(v + EPS) * g + b

        def _mlp_ln(s, W1, b1, W2, b2, g, b):
            h = jax.nn.silu(s @ W1 + b1) @ W2 + b2
            return _ln(h, g, b)
        key = jax.random.key(seed)
        B, S, D = (4, 1024, 512)
        MEM, NOI, RES = (256, 64, 32)
        ks = jax.random.split(key, 40)
        ki = iter(range(40))

        def nrm(shape, scale=0.02):
            return jax.random.normal(ks[next(ki)], shape, jnp.float32) * scale

        def gamma(shape):
            return jnp.ones(shape, jnp.float32) + nrm(shape)
        inp = {'x': jax.random.normal(ks[next(ki)], (B, S, D), jnp.float32), 'pathway_ids': jax.random.randint(ks[next(ki)], (B, S), 0, 500), 'compartment_ids': jax.random.randint(ks[next(ki)], (B, S), 0, 5), 'time_steps': jax.random.randint(ks[next(ki)], (B, S), 0, 5), 'scale_type': jax.random.randint(ks[next(ki)], (B, S), 0, 3), 'memory_state': jax.random.normal(ks[next(ki)], (B, MEM), jnp.float32), 'noise_state': jax.random.normal(ks[next(ki)], (B, NOI), jnp.float32), 'resource_state': jax.random.normal(ks[next(ki)], (B, RES), jnp.float32), 'pw_g': gamma((500, D)), 'pw_b': nrm((500, D)), 'cp_g': gamma((5, D)), 'cp_b': nrm((5, D)), 'tm_g': gamma((5, D)), 'tm_b': nrm((5, D)), 'ms_g': gamma((3, D)), 'ms_b': nrm((3, D)), 'mem_W1': nrm((MEM, D)), 'mem_b1': jnp.zeros((D,)), 'mem_W2': nrm((D, D)), 'mem_b2': jnp.zeros((D,)), 'mem_g': gamma((D,)), 'mem_be': jnp.zeros((D,)), 'noi_W1': nrm((NOI, D)), 'noi_b1': jnp.zeros((D,)), 'noi_W2': nrm((D, D)), 'noi_b2': jnp.zeros((D,)), 'noi_g': gamma((D,)), 'noi_be': jnp.zeros((D,)), 'res_W1': nrm((RES, D)), 'res_b1': jnp.zeros((D,)), 'res_W2': nrm((D, D)), 'res_b2': jnp.zeros((D,)), 'res_g': gamma((D,)), 'res_be': jnp.zeros((D,)), 'int_W1': nrm((6 * D, D)), 'int_b1': jnp.zeros((D,)), 'int_W2': nrm((D, D)), 'int_b2': jnp.zeros((D,)), 'int_g': gamma((D,)), 'int_be': jnp.zeros((D,)), 'aw': jnp.ones((6,), jnp.float32) / 6.0}
        return inp
    _L0_cond_all = _L0_cond_setup()
    _L0_cond_in = {k: v for k, v in _L0_cond_all.items() if k in ('pw_g', 'pw_b', 'cp_g', 'cp_b', 'tm_g', 'tm_b', 'ms_g', 'ms_b', 'mem_W1', 'mem_b1', 'mem_W2', 'mem_b2', 'mem_g', 'mem_be', 'noi_W1', 'noi_b1', 'noi_W2', 'noi_b2', 'noi_g', 'noi_be', 'res_W1', 'res_b1', 'res_W2', 'res_b2', 'res_g', 'res_be', 'int_W1', 'int_b1', 'int_W2', 'int_b2', 'int_g', 'int_be', 'aw')}
    del _L0_cond_all

    def _L1_cond_setup():
        import jax, jax.numpy as jnp
        import numpy as np
        W_DIM = 256
        CLAMP = 256.0
        key = jax.random.key(seed)
        ks = jax.random.split(key, 6)
        B, L, C = (8, 4096, 512)
        return {'x': jax.random.normal(ks[0], (B, L, C), dtype=jnp.float32), 'w': jax.random.normal(ks[1], (B, W_DIM), dtype=jnp.float32), 'weight': jax.random.normal(ks[2], (C, C), dtype=jnp.float32), 'bias': jax.random.normal(ks[3], (C,), dtype=jnp.float32), 'affine_w': jax.random.normal(ks[4], (C, W_DIM), dtype=jnp.float32), 'affine_b': jnp.ones((C,), dtype=jnp.float32)}
    _L1_cond_all = _L1_cond_setup()
    _L1_cond_in = {k: v for k, v in _L1_cond_all.items() if k in ('weight', 'bias', 'affine_w', 'affine_b')}
    del _L1_cond_all
    return {'x': x, 'itok_BxS_0_999': itok_BxS_0_999, 'itok_BxS_0_4': itok_BxS_0_4, 'cond_512': cond_512, 'cond_64': cond_64, 'fside_Bx32_0': fside_Bx32_0, 'mask_BxS_ik0': mask_BxS_ik0, 'L0_cond_pw_g': _L0_cond_in['pw_g'], 'L0_cond_pw_b': _L0_cond_in['pw_b'], 'L0_cond_cp_g': _L0_cond_in['cp_g'], 'L0_cond_cp_b': _L0_cond_in['cp_b'], 'L0_cond_tm_g': _L0_cond_in['tm_g'], 'L0_cond_tm_b': _L0_cond_in['tm_b'], 'L0_cond_ms_g': _L0_cond_in['ms_g'], 'L0_cond_ms_b': _L0_cond_in['ms_b'], 'L0_cond_mem_W1': _L0_cond_in['mem_W1'], 'L0_cond_mem_b1': _L0_cond_in['mem_b1'], 'L0_cond_mem_W2': _L0_cond_in['mem_W2'], 'L0_cond_mem_b2': _L0_cond_in['mem_b2'], 'L0_cond_mem_g': _L0_cond_in['mem_g'], 'L0_cond_mem_be': _L0_cond_in['mem_be'], 'L0_cond_noi_W1': _L0_cond_in['noi_W1'], 'L0_cond_noi_b1': _L0_cond_in['noi_b1'], 'L0_cond_noi_W2': _L0_cond_in['noi_W2'], 'L0_cond_noi_b2': _L0_cond_in['noi_b2'], 'L0_cond_noi_g': _L0_cond_in['noi_g'], 'L0_cond_noi_be': _L0_cond_in['noi_be'], 'L0_cond_res_W1': _L0_cond_in['res_W1'], 'L0_cond_res_b1': _L0_cond_in['res_b1'], 'L0_cond_res_W2': _L0_cond_in['res_W2'], 'L0_cond_res_b2': _L0_cond_in['res_b2'], 'L0_cond_res_g': _L0_cond_in['res_g'], 'L0_cond_res_be': _L0_cond_in['res_be'], 'L0_cond_int_W1': _L0_cond_in['int_W1'], 'L0_cond_int_b1': _L0_cond_in['int_b1'], 'L0_cond_int_W2': _L0_cond_in['int_W2'], 'L0_cond_int_b2': _L0_cond_in['int_b2'], 'L0_cond_int_g': _L0_cond_in['int_g'], 'L0_cond_int_be': _L0_cond_in['int_be'], 'L0_cond_aw': _L0_cond_in['aw'], 'L1_cond_weight': _L1_cond_in['weight'], 'L1_cond_bias': _L1_cond_in['bias'], 'L1_cond_affine_w': _L1_cond_in['affine_w'], 'L1_cond_affine_b': _L1_cond_in['affine_b']}

def reference(x, itok_BxS_0_999, itok_BxS_0_4, cond_512, cond_64, fside_Bx32_0, mask_BxS_ik0, L0_cond_pw_g, L0_cond_pw_b, L0_cond_cp_g, L0_cond_cp_b, L0_cond_tm_g, L0_cond_tm_b, L0_cond_ms_g, L0_cond_ms_b, L0_cond_mem_W1, L0_cond_mem_b1, L0_cond_mem_W2, L0_cond_mem_b2, L0_cond_mem_g, L0_cond_mem_be, L0_cond_noi_W1, L0_cond_noi_b1, L0_cond_noi_W2, L0_cond_noi_b2, L0_cond_noi_g, L0_cond_noi_be, L0_cond_res_W1, L0_cond_res_b1, L0_cond_res_W2, L0_cond_res_b2, L0_cond_res_g, L0_cond_res_be, L0_cond_int_W1, L0_cond_int_b1, L0_cond_int_W2, L0_cond_int_b2, L0_cond_int_g, L0_cond_int_be, L0_cond_aw, L1_cond_weight, L1_cond_bias, L1_cond_affine_w, L1_cond_affine_b):
    import jax
    import jax.numpy as jnp

    def _L0_cond_ref(x, pathway_ids, compartment_ids, time_steps, scale_type, memory_state, noise_state, resource_state, pw_g, pw_b, cp_g, cp_b, tm_g, tm_b, ms_g, ms_b, mem_W1, mem_b1, mem_W2, mem_b2, mem_g, mem_be, noi_W1, noi_b1, noi_W2, noi_b2, noi_g, noi_be, res_W1, res_b1, res_W2, res_b2, res_g, res_be, int_W1, int_b1, int_W2, int_b2, int_g, int_be, aw):
        import jax, jax.numpy as jnp
        import numpy as np
        EPS = 1e-05

        def _ln(x, g, b):
            m = jnp.mean(x, axis=-1, keepdims=True)
            v = jnp.mean((x - m) ** 2, axis=-1, keepdims=True)
            return (x - m) * jax.lax.rsqrt(v + EPS) * g + b

        def _mlp_ln(s, W1, b1, W2, b2, g, b):
            h = jax.nn.silu(s @ W1 + b1) @ W2 + b2
            return _ln(h, g, b)
        h = _ln(x, pw_g[pathway_ids], pw_b[pathway_ids])
        h = _ln(h, cp_g[compartment_ids], cp_b[compartment_ids])
        t = _ln(x, tm_g[time_steps], tm_b[time_steps])
        m = x + _mlp_ln(memory_state, mem_W1, mem_b1, mem_W2, mem_b2, mem_g, mem_be)[:, None, :]
        n = x + _mlp_ln(noise_state, noi_W1, noi_b1, noi_W2, noi_b2, noi_g, noi_be)[:, None, :]
        r = x + _mlp_ln(resource_state, res_W1, res_b1, res_W2, res_b2, res_g, res_be)[:, None, :]
        s = _ln(x, ms_g[scale_type], ms_b[scale_type])
        w = jax.nn.softmax(aw)
        cat = jnp.concatenate([w[0] * h, w[1] * t, w[2] * m, w[3] * n, w[4] * r, w[5] * s], axis=-1)
        return _mlp_ln(cat, int_W1, int_b1, int_W2, int_b2, int_g, int_be)

    def _L1_cond_ref(x, w, weight, bias, affine_w, affine_b):
        import jax, jax.numpy as jnp
        import numpy as np
        W_DIM = 256
        CLAMP = 256.0
        B, L, C = x.shape
        gain = 1.0 / np.sqrt(W_DIM).astype(np.float32)
        styles = w @ (affine_w * gain).T + affine_b
        ws = weight[None, :, :] * styles[:, None, :]
        dcoefs = jax.lax.rsqrt(jnp.sum(ws * ws, axis=2) + 1e-08)
        xm = x * styles[:, None, :]
        y = jnp.einsum('blc,oc->blo', xm, weight)
        y = y * dcoefs[:, None, :]
        y = jnp.clip(y + bias, -CLAMP, CLAMP)
        return y
    x = x + _L0_cond_ref(x, itok_BxS_0_999, itok_BxS_0_4, itok_BxS_0_4, mask_BxS_ik0, cond_512, cond_64, fside_Bx32_0, L0_cond_pw_g, L0_cond_pw_b, L0_cond_cp_g, L0_cond_cp_b, L0_cond_tm_g, L0_cond_tm_b, L0_cond_ms_g, L0_cond_ms_b, L0_cond_mem_W1, L0_cond_mem_b1, L0_cond_mem_W2, L0_cond_mem_b2, L0_cond_mem_g, L0_cond_mem_be, L0_cond_noi_W1, L0_cond_noi_b1, L0_cond_noi_W2, L0_cond_noi_b2, L0_cond_noi_g, L0_cond_noi_be, L0_cond_res_W1, L0_cond_res_b1, L0_cond_res_W2, L0_cond_res_b2, L0_cond_res_g, L0_cond_res_be, L0_cond_int_W1, L0_cond_int_b1, L0_cond_int_W2, L0_cond_int_b2, L0_cond_int_g, L0_cond_int_be, L0_cond_aw)
    x = x + _L1_cond_ref(x, cond_512, L1_cond_weight, L1_cond_bias, L1_cond_affine_w, L1_cond_affine_b)
    return x

_drawn_inputs = setup_inputs


def setup_inputs(seed=0):
    import zlib

    import numpy as np

    out = dict(_drawn_inputs(seed))
    spreads = {'L0_cond_mem_b1': (0.0, 0.473),
     'L0_cond_mem_b2': (0.0, 0.1),
     'L0_cond_mem_be': (0.0, 0.8),
     'L0_cond_noi_b1': (0.0, 0.348),
     'L0_cond_noi_b2': (0.0, 0.1),
     'L0_cond_noi_be': (0.0, 0.764),
     'L0_cond_res_b1': (0.0, 0.427),
     'L0_cond_res_b2': (0.0, 0.1),
     'L0_cond_res_be': (0.0, 0.78),
     'L0_cond_int_b1': (0.0, 0.1),
     'L0_cond_int_b2': (0.0, 0.1),
     'L0_cond_int_be': (0.0, 0.1),
     'L0_cond_aw': (0.1666666716337204, 0.6),
     'L1_cond_affine_b': (1.0, 0.2)}
    factors = {'L0_cond_pw_g': 8.0,
     'L0_cond_pw_b': 8.0,
     'L0_cond_cp_g': 8.0,
     'L0_cond_cp_b': 8.0,
     'L0_cond_tm_g': 8.0,
     'L0_cond_tm_b': 8.0,
     'L0_cond_ms_g': 8.0,
     'L0_cond_ms_b': 8.0,
     'L0_cond_mem_g': 8.0,
     'L0_cond_noi_g': 8.0,
     'L0_cond_res_g': 8.0,
     'L0_cond_int_g': 5.004}
    for name, (base, spread) in spreads.items():
        noise = np.random.default_rng([zlib.crc32(name.encode()), seed]).standard_normal(out[name].shape)
        drawn = base * np.exp(spread * noise) if base else spread * noise
        out[name] = jnp.asarray(drawn.astype(out[name].dtype))
    for name, factor in factors.items():
        out[name] = (out[name] * factor).astype(out[name].dtype)
    return out
```

```python
from contextlib import ExitStack

import concourse.bass as bass
from concourse import mybir

F32 = mybir.dt.float32
F32R = mybir.dt.float32r
BF16 = mybir.dt.bfloat16
I32 = mybir.dt.int32
ALU = mybir.AluOpType
ACT = mybir.ActivationFunctionType
AX = mybir.AxisListType

P = 128
D = 512
C = D // P
BATCH, SEQ = 8, 1024
TILES = BATCH * SEQ // P
PER_BATCH = SEQ // P
KINDS, SCALES = 5, 3
ROWS = BATCH + KINDS + SCALES
PARTS = 3
QUAD = 32
TROWS = PARTS * QUAD
EPS = 1e-5
DEMOD_EPS = 1e-8
CLAMP = 256.0
GAIN = 1.0 / 16.0
UNROLL = 2
FIRST = 4
LAST = TILES - 4


def build(nc, x, sel, idx_pw, idx_kj, pw_table, kj_table, mlp_x, mlp_w1, mlp_w2, mlp_rows, beta_rows,
          b1_rows, int_w1, int_w2, b2_row, norm_rows, aw, weight_t, affine_t, affine_b, eye, sel_cmp, out):
    with ExitStack() as ctx:
        def sb(name, shape, dt=F32):
            return ctx.enter_context(nc.sbuf_tensor(name, shape, dt))

        def sem(name):
            return ctx.enter_context(nc.semaphore(name))

        batch_rows_dram = nc.dram_tensor("batch_rows_dram", (BATCH, 2 * D), F32, kind="Internal").ap()

        wname = ("x", "t", "s", "h", "w2", "l1")
        w_hi = {n: sb(f"w_hi_{n}", [P, C, D], F32R) for n in wname}
        w_lo = {n: sb(f"w_lo_{n}", [P, C, D], F32R) for n in wname}
        norm_g = sb("norm_g", [P, 3, D])
        ident = sb("ident", [P, P])
        row_table = sb("row_table", [TROWS, D], BF16)
        b2_table = sb("b2_table", [TROWS, D], BF16)
        b2_pick = sb("b2_pick", [TROWS, P], BF16)
        cmp = sb("cmp", [TROWS, 1])
        pw_ids = sb("pw_ids", [P, TILES], I32)
        kj_ids = sb("kj_ids", [P, 2, TILES], I32)
        kj_index = sb("kj_index", [P, TILES], I32)
        half = sb("half", [P, D])
        batch_rows = sb("batch_rows", [P, 2, 2 * D])

        work = sb("work", [P, 20 * D])
        place = [0]

        def carve(rows):
            a = place[0]
            place[0] += rows * D
            return work[:, a:a + rows * D].rearrange("p (n d) -> p n d", n=rows)

        gb = [carve(2) for _ in range(2)]
        gk = [carve(3) for _ in range(2)]
        xb = carve(2)
        z = carve(2)
        hid = carve(1)
        vs = carve(1)
        x1 = carve(2)
        yo = carve(2)
        assert place[0] == 20 * D
        xt = sb("xt", [P, 2, D])
        lhs_hi = {n: sb(f"lhs_hi_{n}", [P, C, P], F32R) for n in wname}
        lhs_lo = {n: sb(f"lhs_lo_{n}", [P, C, P], F32R) for n in wname}
        sel_in = sb("sel_in", [TROWS, 2, P], I32)
        onehot = sb("onehot", [TROWS, 2, P], BF16)
        ids_now = sb("ids_now", [P, 4], I32)
        raw = {n: sb(f"raw_{n}", [P, 2, 6]) for n in "xau"}
        mv = {n: sb(f"mv_{n}", [P, 2, 2]) for n in "xau"}
        ve = {n: sb(f"ve_{n}", [P, 2, 1]) for n in "xau"}
        rs = {n: sb(f"rs_{n}", [P, 2, 1]) for n in "xau"}

        stage = [work[:, k * 4 * D:(k + 1) * 4 * D].rearrange("p (c d) -> p c d", c=4) for k in range(5)]
        aff_raw = stage[4][:, 0:2, :]
        style = stage[4][0:QUAD, 2, :]
        dcoef = stage[4][0:QUAD, 3, :]
        affb = xt[0:QUAD, 0, :]
        b1r = xt[0:ROWS, 1, :]
        mx = sb("mx", [P, 4, QUAD])
        mrows = sb("mrows", [TROWS, 4, D])
        mh = sb("mh", [TROWS, D])
        mhT = sb("mhT", [P, C, TROWS])
        rowT = sb("rowT", [P, 6, C, ROWS])
        beta = sb("beta", [ROWS, 3, D])
        sqT = sb("sqT", [P, C, QUAD])
        soft = sb("soft", [P, 4, 8])
        wsm = soft[:, 3, 0:6]
        b2r = beta[0:1, 0, :]

        pre = ctx.enter_context(nc.psum_tensor("pre", [P, 2, D], F32))
        tb = ctx.enter_context(nc.psum_tensor("tb", [P, 4, D], F32))
        pu = ctx.enter_context(nc.psum_tensor("pu", [P, D], F32))
        py = ctx.enter_context(nc.psum_tensor("py", [P, D], F32))

        ld = {n: sem(f"ld_{n}") for n in (
            "aw", "mx", "mw1", "mrows", "beta", "aff", "affb", "b1r", "m0", "m1", "m2", "ident", "norm",
            "cmp", "ids", "l1", "w_m", "w_n", "w_r", "w_h", "w_t", "w_s", "w_w2", "b2")}
        aw_max, aw_exp, aw_ready = sem("aw_max"), sem("aw_exp"), sem("aw_ready")
        mlp1_mm, mlp1_add, mlp_h, h_tr, hT_ready = (sem(n) for n in ("mlp1_mm", "mlp1_add", "mlp_h", "h_tr", "hT_ready"))
        mlp2_mm, c_var, c_rs, c_ready, c_tr, rowT_c = (sem(n) for n in ("mlp2_mm", "c_var", "c_rs", "c_ready", "c_tr", "rowT_c"))
        styles_mm, styles_sq, sq_tr, sqT_ready = (sem(n) for n in ("styles_mm", "styles_sq", "sq_tr", "sqT_ready"))
        wt_sq, dco_mm, dco_in, dco_ready, rows_stored = (sem(n) for n in ("wt_sq", "dco_mm", "dco_in", "dco_ready", "rows_stored"))
        beta_tr, rowT_b = sem("beta_tr"), sem("rowT_b")
        table_mm = {n: sem(f"table_mm_{n}") for n in "hmnrts"}
        hi_done = {n: sem(f"hi_done_{n}") for n in wname}
        lo_done = {n: sem(f"lo_done_{n}") for n in wname}
        wx_sum = sem("wx_sum")
        dve_step = sem("dve_step")
        half_set, kj_ready = sem("half_set"), sem("kj_ready")
        prologue_done = sem("prologue_done")

        x_loaded = [sem(f"x_loaded_{u}") for u in range(2)]
        sel_loaded = [sem(f"sel_loaded_{u}") for u in range(2)]
        gb_loaded = [sem(f"gb_loaded_{u}") for u in range(2)]
        gk_loaded = [sem(f"gk_loaded_{u}") for u in range(2)]
        out_stored = [sem(f"out_stored_{u}") for u in range(2)]
        rows_loaded = sem("rows_loaded")
        ids_copied = sem("ids_copied")
        stats = {n: sem(f"stats_{n}") for n in "xau"}
        meanvar = {n: sem(f"meanvar_{n}") for n in "xau"}
        var_ready = {n: sem(f"var_ready_{n}") for n in "xau"}
        rstd_ready = {n: sem(f"rstd_ready_{n}") for n in "xau"}
        z_ready, zg_ready, a_ready, zh_ready = sem("z_ready"), sem("zg_ready"), sem("a_ready"), sem("zh_ready")
        t_ready, s_ready, h_ready = sem("t_ready"), sem("s_ready"), sem("h_ready")
        xb_ready, onehot_ready = sem("xb_ready"), sem("onehot_ready")
        turned = {n: sem(f"turned_{n}") for n in wname}
        hi_ready = {n: sem(f"hi_ready_{n}") for n in wname}
        lo_ready = {n: sem(f"lo_ready_{n}") for n in wname}
        mm_done = {n: sem(f"mm_done_{n}") for n in wname}
        hid_ready, v_ready, x1_ready, x1s_ready = sem("hid_ready"), sem("v_ready"), sem("x1_ready"), sem("x1s_ready")
        ys_ready, yb_ready, yc_ready, out_ready = sem("ys_ready"), sem("yb_ready"), sem("yc_ready"), sem("out_ready")

        def at_least(eng, s, n):
            if not isinstance(n, int) or n > 0:
                eng.wait_ge(s, n)

        def loaded(eng, sems, t, u):
            eng.wait_ge(sems[u], (t - u) * 8 + 16)

        def apart(eng):
            eng.wait_ge(prologue_done, 1)

        def value(eng, n):
            return n if isinstance(n, int) else eng.to_reg(n)

        def batch_of(t):
            return t // PER_BATCH

        def batch_slot(t, what):
            b = batch_of(t) % 2
            if isinstance(t, int):
                return batch_rows[:, b, what * D:(what + 1) * D]
            return batch_rows[:].rearrange("p b d -> p (b d)")[:, bass.ds(b * (2 * D) + what * D, D)]

        def iterate(eng, body):
            for i in range(-1, FIRST):
                body(i, i % 2)
            with eng.Fori(FIRST, LAST, UNROLL) as i:
                for k in range(UNROLL):
                    body(i + k, k)
            for i in range(LAST, TILES + 2):
                body(i, i % 2)

        def has(t):
            return not isinstance(t, int) or 0 <= t < TILES

        def w1_part(k):
            return int_w1[k * D:(k + 1) * D, :].rearrange("(c p) d -> p c d", p=P)

        block = ctx.enter_context(nc.Block())

        @block.sync
        def _(sp):
            sp.dma_start(soft[:, 0, 0:6], aw.rearrange("(a k) -> a k", a=1).to_broadcast([P, 6])).then_inc(ld["aw"], 16)
            sp.dma_start(mx[:], mlp_x).then_inc(ld["mx"], 16)
            sp.dma_start(stage[3], mlp_w1).then_inc(ld["mw1"], 16)
            sp.dma_start(mrows[:], mlp_rows).then_inc(ld["mrows"], 16)
            sp.dma_start(ident[:], eye).then_inc(ld["ident"], 16)
            sp.dma_start(aff_raw, affine_t.rearrange("(c p) d -> p c d", p=P)).then_inc(ld["aff"], 16)
            sp.dma_start(affb, affine_b).then_inc(ld["affb"], 16)
            sp.dma_start(beta[:], beta_rows).then_inc(ld["beta"], 16)
            for m in range(3):
                sp.dma_start(stage[m], mlp_w2[m].rearrange("(c p) d -> p c d", p=P)).then_inc(ld[f"m{m}"], 16)
            sp.wait_ge(mlp1_mm, 1)
            sp.dma_start(stage[3], weight_t.rearrange("(c p) d -> p c d", p=P)).then_inc(ld["l1"], 16)
            sp.dma_start(b1r, b1_rows).then_inc(ld["b1r"], 16)
            sp.dma_start(norm_g[:], norm_rows.rearrange("(a k) d -> a k d", a=1).to_broadcast([P, 3, D])).then_inc(ld["norm"], 16)
            sp.dma_start(cmp[:], sel_cmp).then_inc(ld["cmp"], 16)
            sp.dma_start(pw_ids[:], idx_pw).then_inc(ld["ids"], 16)
            sp.dma_start(kj_ids[:], idx_kj).then_inc(ld["ids"], 16)
            sp.wait_ge(mlp2_mm, 1)
            sp.dma_start(stage[0], w1_part(2)).then_inc(ld["w_m"], 16)
            sp.dma_start(stage[1], w1_part(3)).then_inc(ld["w_n"], 16)
            sp.dma_start(stage[2], w1_part(4)).then_inc(ld["w_r"], 16)
            sp.wait_ge(rowT_b, 1)
            sp.dma_start(b2r, b2_row).then_inc(ld["b2"], 16)
            sp.wait_ge(dco_mm, 1)
            sp.dma_start(stage[3], w1_part(0)).then_inc(ld["w_h"], 16)
            sp.wait_ge(wx_sum, 1)
            sp.wait_ge(table_mm["r"], 1)
            sp.dma_start(stage[1], w1_part(1)).then_inc(ld["w_t"], 16)
            sp.dma_start(stage[2], w1_part(5)).then_inc(ld["w_s"], 16)
            sp.wait_ge(lo_done["x"], 1)
            sp.dma_start(stage[0], int_w2.rearrange("(c p) d -> p c d", p=P)).then_inc(ld["w_w2"], 16)
            sp.wait_ge(dco_ready, 1)
            sp.dma_start(batch_rows_dram[:, 0:D], style[0:BATCH, :]).then_inc(rows_stored, 16)
            sp.dma_start(batch_rows_dram[:, D:2 * D], dcoef[0:BATCH, :]).then_inc(rows_stored, 16)
            sp.wait_ge(rows_stored, 32)

            def load(t, u):
                apart(sp)
                at_least(sp, z_ready, t - 1)
                at_least(sp, xb_ready, t - 1)
                at_least(sp, turned["x"], t - 1)
                sp.dma_start(xt[:, u, :], x[bass.ds(t * P, P), :]).then_inc(x_loaded[u], 16)
                apart(sp)
                at_least(sp, onehot_ready, t - 1)
                sp.dma_start(sel_in[:, u, :], sel[:, bass.ds(t * P, P)]).then_inc(sel_loaded[u], 16)

            def load_rows(b):
                apart(sp)
                at_least(sp, ys_ready, (b - 1) * PER_BATCH)
                at_least(sp, x1s_ready, (b - 1) * PER_BATCH)
                if isinstance(b, int):
                    place = batch_rows[:, b % 2, :]
                else:
                    place = batch_rows[:].rearrange("p b d -> p (b d)")[:, bass.ds((b % 2) * (2 * D), 2 * D)]
                sp.dma_start(place, batch_rows_dram[bass.ds(b, 1), :].to_broadcast([P, 2 * D])).then_inc(rows_loaded, 16)

            def store(t, u):
                apart(sp)
                sp.wait_ge(out_ready, t + 1)
                sp.dma_start(out[bass.ds(t * P, P), :], yo[:, u, :]).then_inc(out_stored[u], 16)

            sp.wait_ge(prologue_done, 1)
            load(0, 0)
            load(1, 1)

            def step(i, u):
                if has(i + 2):
                    load(i + 2, u)
                if has(i - 2):
                    store(i - 2, u)

            load_rows(0)
            for i in range(PER_BATCH):
                step(i, i % 2)
            with sp.Fori(1, BATCH - 1) as b:
                load_rows(b)
                with sp.Fori(0, PER_BATCH, UNROLL) as k:
                    for u in range(UNROLL):
                        step(b * PER_BATCH + k + u, u)
            load_rows(BATCH - 1)
            for i in range(TILES - PER_BATCH, TILES + 2):
                step(i, i % 2)
            for u in range(2):
                sp.wait_ge(out_stored[u], 8 * TILES)

        @block.gpsimd
        def _(pool):
            nc.gpsimd.memset(half[:], -0.5).then_inc(half_set, 1)
            pool.wait_ge(half_set, 1)
            pool.wait_ge(c_var, 1)
            nc.gpsimd.tensor_tensor(rs["u"][0:TROWS, 0, :], ve["u"][0:TROWS, 0, :], half[0:TROWS, 0:1], ALU.pow).then_inc(c_rs, 1)
            pool.wait_ge(dco_in, 1)
            nc.gpsimd.tensor_tensor(dcoef, dcoef, half[0:QUAD, :], ALU.pow).then_inc(dco_ready, 1)
            pool.wait_ge(prologue_done, 1)
            pool.wait_ge(rows_stored, 32)
            pool.wait_ge(kj_ready, 1)
            pool.wait_ge(ld["ids"], 32)

            def gather(t, u):
                at_least(pool, h_ready, t - 1)
                at_least(pool, turned["h"], t - 1)
                count = value(pool, 2 * t + 2)
                nc.gpsimd.tensor_copy(ids_now[:, u:u + 1], pw_ids[:, bass.ds(t, 1)]).then_inc(ids_copied, 1)
                nc.gpsimd.tensor_copy(ids_now[:, 2 + u:3 + u], kj_index[:, bass.ds(t, 1)]).then_inc(ids_copied, 1)
                apart(pool)
                pool.wait_ge(ids_copied, count)
                pool.indirect_dma_start(gb[u].rearrange("p n d -> p (n d)"), None, pw_table,
                                        bass.IndirectOffsetOnAxis(ids_now[:, u:u + 1], 0)).then_inc(gb_loaded[u], 16)
                pool.indirect_dma_start(gk[u].rearrange("p n d -> p (n d)"), None, kj_table,
                                        bass.IndirectOffsetOnAxis(ids_now[:, 2 + u:3 + u], 0)).then_inc(gk_loaded[u], 16)

            def rstd(n, t, u):
                pool.wait_ge(var_ready[n], t + 1)
                nc.gpsimd.tensor_tensor(rs[n][:, u, :], ve[n][:, u, :], half[:, 0:1], ALU.pow).then_inc(rstd_ready[n], 1)

            gather(0, 0)

            def body(i, u):
                f, v = i + 1, 1 - u
                if has(f):
                    rstd("x", f, v)
                    pool.wait_ge(z_ready, f + 1)
                    loaded(pool, gb_loaded, f, v)
                    nc.gpsimd.tensor_tensor(gb[v][:, 0, :], z[:, v, :], gb[v][:, 0, :], ALU.mult).then_inc(zg_ready, 1)
                    pool.wait_ge(zg_ready, f + 1)
                    nc.gpsimd.tensor_tensor(gb[v][:, 0, :], gb[v][:, 0, :], gb[v][:, 1, :], ALU.add).then_inc(a_ready, 1)
                    rstd("a", f, v)
                if has(i + 2):
                    gather(i + 2, u)
                if has(i - 1):
                    rstd("u", i - 1, v)
                if has(i - 2):
                    t = i - 2
                    pool.wait_ge(ys_ready, t + 1)
                    nc.gpsimd.tensor_tensor(yo[:, u, :], yo[:, u, :], norm_g[:, 2, :], ALU.add).then_inc(yb_ready, 1)
                    apart(pool)
                    pool.wait_ge(yb_ready, t + 1)
                    nc.gpsimd.tensor_scalar(yo[:, u, :], yo[:, u, :], CLAMP, -CLAMP, ALU.min, ALU.max).then_inc(yc_ready, 1)
                    pool.wait_ge(yc_ready, t + 1)
                    nc.gpsimd.tensor_tensor(yo[:, u, :], yo[:, u, :], x1[:, u, :], ALU.add).then_inc(out_ready, 1)
                if has(i - 1):
                    t = i - 1
                    pool.wait_ge(x1_ready, t + 1)
                    pool.wait_ge(rows_loaded, batch_of(t) * 16 + 16)
                    nc.gpsimd.tensor_tensor(vs[:, 0, :], x1[:, v, :], batch_slot(t, 0), ALU.mult).then_inc(x1s_ready, 1)
                if has(f):
                    loaded(pool, x_loaded, f, v)
                    at_least(pool, x1_ready, f - 1)
                    nc.gpsimd.tensor_tensor(xb[:, v, :], xt[:, v, :], norm_g[:, 1, :], ALU.add).then_inc(xb_ready, 1)

            iterate(pool, body)

        @block.scalar
        def _(act):
            act.wait_ge(aw_max, 1)
            nc.scalar.activation(soft[:, 1, 0:6], soft[:, 0, 0:6], ACT.Exp, bias=soft[:, 2, 0:1]).then_inc(aw_exp, 1)
            act.wait_ge(mlp1_add, 1)
            nc.scalar.activation(mh[:], mh[:], ACT.Silu).then_inc(mlp_h, 1)

            def high(n, k, scale=None):
                nc.scalar.activation(w_hi[n][:], stage[k], ACT.Copy, scale=1.0 if scale is None else scale).then_inc(hi_done[n], 1)

            act.wait_ge(ld["l1"], 16)
            high("l1", 3)
            act.wait_ge(wx_sum, 1)
            high("x", 0)
            act.wait_ge(ld["w_h"], 16)
            high("h", 3, wsm[:, 0:1])
            act.wait_ge(ld["w_t"], 16)
            high("t", 1, wsm[:, 1:2])
            act.wait_ge(ld["w_s"], 16)
            high("s", 2, wsm[:, 5:6])
            act.wait_ge(ld["w_w2"], 16)
            high("w2", 0)

            def split(n, bank, t):
                act.wait_ge(turned[n], t + 1)
                at_least(act, mm_done[n], t)
                nc.scalar.activation(lhs_hi[n][:].rearrange("p c t -> p (c t)"), tb[:, bank, :], ACT.Copy).then_inc(hi_ready[n], 1)

            def body(i, u):
                if has(i - 1):
                    split("w2", 0, i - 1)
                if has(i):
                    split("s", 1, i)
                if has(i - 2):
                    split("l1", 2, i - 2)
                if has(i):
                    split("h", 3, i)
                if has(i + 1):
                    split("x", 0, i + 1)
                    split("t", 1, i + 1)
                if has(i):
                    act.wait_ge(mm_done["h"], i + 1)
                    at_least(act, turned["w2"], i)
                    if isinstance(i, int) and i == 0:
                        act.wait_ge(prologue_done, 1)
                    nc.scalar.activation(hid[:, 0, :], pre[:, u, :], ACT.Silu).then_inc(hid_ready, 1)

            iterate(act, body)

        @block.vector
        def _(dve):
            steps = [0]

            def link(ins):
                steps[0] += 1
                ins.then_inc(dve_step, 1)
                dve.wait_ge(dve_step, steps[0])

            dve.wait_ge(ld["aw"], 16)
            link(nc.vector.tensor_reduce(soft[:, 2, 1:2], soft[:, 0, 0:6], AX.X, ALU.max))
            nc.vector.tensor_scalar(soft[:, 2, 0:1], soft[:, 2, 1:2], -1.0, None, ALU.mult).then_inc(aw_max, 1)
            dve.wait_ge(aw_exp, 1)
            link(nc.vector.tensor_reduce(soft[:, 2, 2:3], soft[:, 1, 0:6], AX.X, ALU.add))
            link(nc.vector.reciprocal(soft[:, 2, 3:4], soft[:, 2, 2:3]))
            nc.vector.tensor_scalar(wsm, soft[:, 1, 0:6], soft[:, 2, 3:4], None, ALU.mult).then_inc(aw_ready, 1)
            nc.vector.memset(row_table[:], 0.0)
            nc.vector.memset(b2_table[:], 0.0)
            nc.vector.memset(rowT[:], 0.0)
            link(nc.vector.memset(b2_pick[:], 0.0))
            for k in range(PARTS):
                link(nc.vector.memset(b2_pick[QUAD * k:QUAD * k + 1, :], 1.0))
            dve.wait_ge(mlp1_mm, 1)
            dve.wait_ge(ld["mrows"], 16)
            nc.vector.tensor_tensor(mh[:], pu[0:TROWS, :], mrows[:, 0, :], ALU.add).then_inc(mlp1_add, 1)
            dve.wait_ge(styles_mm, 1)
            dve.wait_ge(ld["affb"], 16)
            link(nc.vector.scalar_tensor_tensor(out=style, in0=pre[0:QUAD, 1, :], scalar=GAIN, in1=affb, op0=ALU.mult, op1=ALU.add))
            nc.vector.tensor_tensor(dcoef, style, style, ALU.mult).then_inc(styles_sq, 1)
            dve.wait_ge(beta_tr, 1)
            dve.wait_ge(aw_ready, 1)
            for k, unit in enumerate((0, 1, 5)):
                src = tb[:, 2, k * C * ROWS:(k + 1) * C * ROWS].rearrange("p (c r) -> p c r", c=C)
                link(nc.vector.tensor_scalar(rowT[:, unit, :, :], src, wsm[:, unit:unit + 1], None, ALU.mult))
            nc.vector.tensor_copy(soft[:, 2, 4:5], wsm[:, 0:1]).then_inc(rowT_b, 1)
            dve.wait_ge(h_tr, 1)
            nc.vector.tensor_copy(mhT[:].rearrange("p c r -> p (c r)"), tb[:, 0, 0:C * TROWS]).then_inc(hT_ready, 1)
            dve.wait_ge(sq_tr, 1)
            nc.vector.tensor_copy(sqT[:].rearrange("p c r -> p (c r)"), tb[:, 3, 0:C * QUAD]).then_inc(sqT_ready, 1)
            dve.wait_ge(hi_done["l1"], 1)
            link(nc.vector.tensor_tensor(w_lo["l1"][:], stage[3], w_hi["l1"][:].bitcast(F32), ALU.subtract))
            nc.vector.tensor_tensor(stage[3], stage[3], stage[3], ALU.mult).then_inc(wt_sq, 1)
            dve.wait_ge(mlp2_mm, 1)
            link(nc.vector.tensor_tensor(mh[:], py[0:TROWS, :], mrows[:, 1, :], ALU.add))
            link(nc.vector.bn_stats(raw["u"][0:TROWS, 0, :], mh[:]))
            link(nc.vector.bn_aggr(mv["u"][0:TROWS, 0, :], raw["u"][0:TROWS, 0, :]))
            nc.vector.tensor_scalar(ve["u"][0:TROWS, 0, :], mv["u"][0:TROWS, 0, 1:2], EPS, None, ALU.add).then_inc(c_var, 1)
            dve.wait_ge(c_rs, 1)
            link(nc.vector.tensor_scalar(mh[:], mh[:], mv["u"][0:TROWS, 0, 0:1], rs["u"][0:TROWS, 0, :], ALU.subtract, ALU.mult))
            link(nc.vector.tensor_tensor(mh[:], mh[:], mrows[:, 2, :], ALU.mult))
            nc.vector.tensor_tensor(mh[:], mh[:], mrows[:, 3, :], ALU.add).then_inc(c_ready, 1)
            dve.wait_ge(dco_mm, 1)
            nc.vector.tensor_scalar(dcoef, pre[0:QUAD, 1, :], DEMOD_EPS, None, ALU.add).then_inc(dco_in, 1)
            dve.wait_ge(c_tr, 1)
            for m in range(3):
                src = tb[:, 1, 0:C * TROWS].rearrange("p (c r) -> p c r", c=C)[:, :, QUAD * m:QUAD * m + BATCH]
                link(nc.vector.tensor_scalar(rowT[:, 2 + m, :, 0:BATCH], src, wsm[:, 2 + m:3 + m], None, ALU.mult))
            nc.vector.tensor_copy(soft[:, 2, 5:6], wsm[:, 0:1]).then_inc(rowT_c, 1)
            dve.wait_ge(ld["w_m"], 16)
            dve.wait_ge(table_mm["m"], 1)
            link(nc.vector.tensor_scalar(stage[0], stage[0], wsm[:, 2:3], None, ALU.mult))
            dve.wait_ge(ld["w_n"], 16)
            link(nc.vector.scalar_tensor_tensor(out=stage[0].rearrange("p c d -> p (c d)"), in0=stage[1].rearrange("p c d -> p (c d)"),
                                                scalar=wsm[:, 3:4], in1=stage[0].rearrange("p c d -> p (c d)"), op0=ALU.mult, op1=ALU.add))
            dve.wait_ge(ld["w_r"], 16)
            nc.vector.scalar_tensor_tensor(out=stage[0].rearrange("p c d -> p (c d)"), in0=stage[2].rearrange("p c d -> p (c d)"),
                                           scalar=wsm[:, 4:5], in1=stage[0].rearrange("p c d -> p (c d)"), op0=ALU.mult, op1=ALU.add).then_inc(wx_sum, 1)

            def low(n, k, scale):
                dve.wait_ge(hi_done[n], 1)
                flat = "p c d -> p (c d)"
                nc.vector.scalar_tensor_tensor(out=w_lo[n][:].rearrange(flat), in0=stage[k].rearrange(flat), scalar=scale,
                                               in1=w_hi[n][:].bitcast(F32).rearrange(flat), op0=ALU.mult, op1=ALU.subtract).then_inc(lo_done[n], 1)

            low("x", 0, 1.0)
            low("h", 3, wsm[:, 0:1])
            low("t", 1, wsm[:, 1:2])
            low("s", 2, wsm[:, 5:6])
            low("w2", 0, 1.0)

            def three_parts(table, src, rows):
                for k in range(PARTS):
                    part = table[QUAD * k:QUAD * k + rows, :]
                    link(nc.vector.tensor_copy(part, src))
                    if k + 1 < PARTS:
                        link(nc.vector.tensor_copy(mh[0:rows, :], part))
                        link(nc.vector.tensor_tensor(src, src, mh[0:rows, :], ALU.subtract))

            dve.wait_ge(ld["b2"], 16)
            three_parts(b2_table, b2r, 1)
            dve.wait_ge(table_mm["s"], 1)
            dve.wait_ge(ld["b1r"], 16)
            link(nc.vector.tensor_tensor(b1r, pre[0:ROWS, 0, :], b1r, ALU.add))
            three_parts(row_table, b1r, ROWS)
            dve.wait_ge(ld["ids"], 32)
            nc.vector.scalar_tensor_tensor(out=kj_index[:], in0=kj_ids[:, 0, :], scalar=float(SCALES), in1=kj_ids[:, 1, :],
                                           op0=ALU.mult, op1=ALU.add).then_inc(kj_ready, 1)
            dve.wait_ge(lo_done["w2"], 1)
            dve.wait_ge(ld["norm"], 16)
            dve.wait_ge(ld["cmp"], 16)
            nc.vector.tensor_copy(soft[:, 2, 6:7], wsm[:, 0:1]).then_inc(prologue_done, 1)
            dve.wait_ge(rows_stored, 32)

            def moments(n, src, t, u):
                count = value(dve, t + 1)
                nc.vector.bn_stats(raw[n][:, u, :], src).then_inc(stats[n], 1)
                apart(dve)
                dve.wait_ge(stats[n], count)
                nc.vector.bn_aggr(mv[n][:, u, :], raw[n][:, u, :]).then_inc(meanvar[n], 1)
                dve.wait_ge(meanvar[n], t + 1)
                nc.vector.tensor_scalar(ve[n][:, u, :], mv[n][:, u, 1:2], EPS, None, ALU.add).then_inc(var_ready[n], 1)

            def low_part(n, bank, t):
                dve.wait_ge(hi_ready[n], t + 1)
                nc.vector.tensor_tensor(lhs_lo[n][:].rearrange("p c t -> p (c t)"), tb[:, bank, :],
                                        lhs_hi[n][:].rearrange("p c t -> p (c t)").bitcast(F32), ALU.subtract).then_inc(lo_ready[n], 1)

            def body(i, u):
                f, v = i + 1, 1 - u
                if has(f):
                    loaded(dve, x_loaded, f, v)
                    moments("x", xt[:, v, :], f, v)
                if has(i - 1):
                    low_part("w2", 0, i - 1)
                if has(f):
                    dve.wait_ge(rstd_ready["x"], f + 1)
                    at_least(dve, zg_ready, f - 1)
                    at_least(dve, s_ready, f - 1)
                    nc.vector.tensor_scalar(z[:, v, :], xt[:, v, :], mv["x"][:, v, 0:1], rs["x"][:, v, :],
                                            ALU.subtract, ALU.mult).then_inc(z_ready, 1)
                if has(i):
                    low_part("s", 1, i)
                if has(f):
                    dve.wait_ge(z_ready, f + 1)
                    loaded(dve, gk_loaded, f, v)
                    nc.vector.tensor_tensor(gk[v][:, 1, :], z[:, v, :], gk[v][:, 1, :], ALU.mult).then_inc(t_ready, 1)
                    nc.vector.tensor_tensor(gk[v][:, 2, :], z[:, v, :], gk[v][:, 2, :], ALU.mult).then_inc(s_ready, 1)
                    loaded(dve, sel_loaded, f, v)
                    at_least(dve, mm_done["h"], f - 1)
                    nc.vector.tensor_scalar(onehot[:, v, :], sel_in[:, v, :], cmp[:, 0:1], None, ALU.is_equal).then_inc(onehot_ready, 1)
                if has(i - 2):
                    low_part("l1", 2, i - 2)
                if has(i):
                    low_part("h", 3, i)
                if has(f):
                    dve.wait_ge(a_ready, f + 1)
                    moments("a", gb[v][:, 0, :], f, v)
                if has(i - 1):
                    dve.wait_ge(mm_done["w2"], i)
                    moments("u", pu[:], i - 1, v)
                if has(f):
                    dve.wait_ge(rstd_ready["a"], f + 1)
                    nc.vector.tensor_scalar(gb[v][:, 0, :], gb[v][:, 0, :], mv["a"][:, v, 0:1], rs["a"][:, v, :],
                                            ALU.subtract, ALU.mult).then_inc(zh_ready, 1)
                    dve.wait_ge(zh_ready, f + 1)
                    nc.vector.tensor_tensor(gk[v][:, 0, :], gb[v][:, 0, :], gk[v][:, 0, :], ALU.mult).then_inc(h_ready, 1)
                if has(i - 1):
                    t = i - 1
                    at_least(dve, turned["l1"], t)
                    nc.vector.scalar_tensor_tensor(out=vs[:, 0, :], in0=pu[:], scalar=mv["u"][:, v, 0:1], in1=norm_g[:, 0, :],
                                                   op0=ALU.subtract, op1=ALU.mult).then_inc(v_ready, 1)
                    dve.wait_ge(rstd_ready["u"], t + 1)
                    dve.wait_ge(v_ready, t + 1)
                    dve.wait_ge(xb_ready, t + 1)
                    at_least(dve, out_ready, t - 1)
                    nc.vector.scalar_tensor_tensor(out=x1[:, v, :], in0=vs[:, 0, :], scalar=rs["u"][:, v, :], in1=xb[:, v, :],
                                                   op0=ALU.mult, op1=ALU.add).then_inc(x1_ready, 1)
                if has(i - 2):
                    t = i - 2
                    dve.wait_ge(mm_done["l1"], t + 1)
                    dve.wait_ge(rows_loaded, batch_of(t) * 16 + 16)
                    if not isinstance(t, int) or t >= 2:
                        loaded(dve, out_stored, t - 2, u)
                    nc.vector.tensor_tensor(yo[:, u, :], py[:], batch_slot(t, 1), ALU.mult).then_inc(ys_ready, 1)
                if has(f):
                    low_part("x", 0, f)
                    low_part("t", 1, f)

            iterate(dve, body)

        @block.tensor
        def _(pe):
            for n in ("mx", "mw1"):
                pe.wait_ge(ld[n], 16)
            for m, chunks in enumerate(((0, 1), (2,), (3,))):
                for c in chunks:
                    last = pe.matmul(pu[QUAD * m:QUAD * (m + 1), :], mx[:, c, :], stage[3][:, c, :],
                                     start=c == chunks[0], stop=c == chunks[-1])
            last.then_inc(mlp1_mm, 1)
            pe.wait_ge(ld["aff"], 16)
            for c in range(2):
                last = pe.matmul(pre[0:QUAD, 1, :], mx[:, c, :], aff_raw[:, c, :], start=c == 0, stop=c == 1)
            last.then_inc(styles_mm, 1)
            pe.wait_ge(ld["ident"], 16)
            pe.wait_ge(ld["beta"], 16)
            for k in range(3):
                for c in range(C):
                    at = (k * C + c) * ROWS
                    last = pe.transpose(tb[:, 2, at:at + ROWS], beta[:, k, c * P:(c + 1) * P], ident[0:ROWS, 0:ROWS])
            last.then_inc(beta_tr, 1)
            pe.wait_ge(mlp_h, 1)
            for c in range(C):
                last = pe.transpose(tb[:, 0, c * TROWS:(c + 1) * TROWS], mh[:, c * P:(c + 1) * P], ident[0:TROWS, 0:TROWS])
            last.then_inc(h_tr, 1)
            pe.wait_ge(styles_sq, 1)
            for c in range(C):
                last = pe.transpose(tb[:, 3, c * QUAD:(c + 1) * QUAD], dcoef[:, c * P:(c + 1) * P], ident[0:QUAD, 0:QUAD])
            last.then_inc(sq_tr, 1)
            pe.wait_ge(hT_ready, 1)
            for m in range(3):
                pe.wait_ge(ld[f"m{m}"], 16)
                for c in range(C):
                    last = pe.matmul(py[QUAD * m:QUAD * (m + 1), :], mhT[:, c, QUAD * m:QUAD * (m + 1)], stage[m][:, c, :],
                                     start=c == 0, stop=c == C - 1)
            last.then_inc(mlp2_mm, 1)
            pe.wait_ge(sqT_ready, 1)
            pe.wait_ge(wt_sq, 1)
            for c in range(C):
                last = pe.matmul(pre[0:QUAD, 1, :], sqT[:, c, :], stage[3][:, c, :], start=c == 0, stop=c == C - 1)
            last.then_inc(dco_mm, 1)
            pe.wait_ge(c_ready, 1)
            for c in range(C):
                last = pe.transpose(tb[:, 1, c * TROWS:(c + 1) * TROWS], mh[:, c * P:(c + 1) * P], ident[0:TROWS, 0:TROWS])
            last.then_inc(c_tr, 1)
            pe.wait_ge(rowT_b, 1)
            pe.wait_ge(rowT_c, 1)
            order = (("m", 2, 0), ("n", 3, 1), ("r", 4, 2), ("h", 0, 3), ("t", 1, 1), ("s", 5, 2))
            for n, unit, k in order:
                pe.wait_ge(ld[f"w_{n}"], 16)
                for c in range(C):
                    last = pe.matmul(pre[0:ROWS, 0, :], rowT[:, unit, c, :], stage[k][:, c, :],
                                     start=n == "m" and c == 0, stop=n == "s" and c == C - 1)
                last.then_inc(table_mm[n], 1)
            pe.wait_ge(prologue_done, 1)

            def turn(n, bank, src):
                for c in range(C):
                    last = pe.transpose(tb[:, bank, c * P:(c + 1) * P], src[:, c * P:(c + 1) * P], ident[:])
                last.then_inc(turned[n], 1)

            def unit(n, dst, start, stop):
                passes = ((lhs_hi, w_hi), (lhs_hi, w_lo), (lhs_lo, w_hi))
                for c in range(C):
                    for k, (a, b) in enumerate(passes):
                        last = pe.matmul(dst, a[n][:, c, :], b[n][:, c, :], start=start and c == 0 and k == 0,
                                         stop=stop and c == C - 1 and k == 2)
                last.then_inc(mm_done[n], 1)

            def body(i, u):
                v = 1 - u
                if has(i):
                    at_least(pe, hid_ready, i - 1)
                    pe.wait_ge(lo_ready["x"], i + 1)
                    unit("x", pre[:, u, :], True, False)
                if has(i - 1):
                    pe.wait_ge(hid_ready, i)
                    at_least(pe, lo_ready["x"], min(i + 1, TILES) if isinstance(i, int) else i + 1)
                    turn("w2", 0, hid[:, 0, :])
                if has(i):
                    pe.wait_ge(s_ready, i + 1)
                    pe.wait_ge(lo_ready["t"], i + 1)
                    turn("s", 1, gk[u][:, 2, :])
                    unit("t", pre[:, u, :], False, False)
                if has(i - 2):
                    pe.wait_ge(x1s_ready, i - 1)
                    at_least(pe, lo_ready["l1"], i - 2)
                    turn("l1", 2, vs[:, 0, :])
                if has(i):
                    pe.wait_ge(h_ready, i + 1)
                    at_least(pe, lo_ready["h"], i)
                    turn("h", 3, gk[u][:, 0, :])
                if has(i - 1):
                    pe.wait_ge(lo_ready["w2"], i)
                    at_least(pe, v_ready, i - 1)
                    pe.matmul(pu[:], b2_pick[:], b2_table[:], start=True, stop=False)
                    unit("w2", pu[:], False, True)
                if has(i - 2):
                    pe.wait_ge(lo_ready["l1"], i - 1)
                    at_least(pe, ys_ready, i - 2)
                    unit("l1", py[:], True, True)
                if has(i + 1):
                    loaded(pe, x_loaded, i + 1, v)
                    turn("x", 0, xt[:, v, :])
                if has(i):
                    pe.wait_ge(lo_ready["s"], i + 1)
                    unit("s", pre[:, u, :], False, False)
                if has(i + 1):
                    pe.wait_ge(t_ready, i + 2)
                    turn("t", 1, gk[v][:, 1, :])
                if has(i):
                    pe.wait_ge(onehot_ready, i + 1)
                    pe.matmul(pre[:, u, :], onehot[:, u, :], row_table[:], start=False, stop=False)
                    pe.wait_ge(lo_ready["h"], i + 1)
                    unit("h", pre[:, u, :], False, True)

            iterate(pe, body)


def kernel(**inputs):
    import numpy as np
    import concourse.bacc as bacc
    from concourse.bass_utils import run_bass_kernel_spmd

    a = {k: np.asarray(v) for k, v in inputs.items()}
    g = {k[len("L0_cond_"):]: v for k, v in a.items() if k.startswith("L0_cond_")}
    f32 = np.float32

    def by_tile(ids):
        return ids.reshape(TILES, P).T

    kinds, scales = a["itok_BxS_0_4"], a["mask_BxS_ik0"]
    sel = np.full((TROWS, BATCH * SEQ), -1, np.int32)
    cmp = np.zeros((TROWS, 1), f32)
    for k in range(PARTS):
        r = QUAD * k
        sel[r:r + BATCH] = np.repeat(np.arange(BATCH, dtype=np.int32), SEQ)
        sel[r + BATCH:r + BATCH + KINDS] = kinds.reshape(-1)
        sel[r + BATCH + KINDS:r + ROWS] = scales.reshape(-1)
        cmp[r:r + ROWS, 0] = [*range(BATCH), *range(KINDS), *range(SCALES)]
    mlp_x = np.zeros((P, 4, QUAD), f32)
    mlp_x[:, 0:2, 0:BATCH] = a["cond_512"].T.reshape(2, P, BATCH).transpose(1, 0, 2)
    mlp_x[0:64, 2, 0:BATCH] = a["cond_64"].T
    mlp_x[0:32, 3, 0:BATCH] = a["fside_Bx32_0"].T
    mlp_w1 = np.zeros((P, 4, D), f32)
    mlp_w1[:, 0:2] = g["mem_W1"].reshape(2, P, D).transpose(1, 0, 2)
    mlp_w1[0:64, 2] = g["noi_W1"]
    mlp_w1[0:32, 3] = g["res_W1"]
    mlp_rows = np.zeros((TROWS, 4, D), f32)
    for m, n in enumerate(("mem", "noi", "res")):
        for k, row in enumerate(("b1", "b2", "g", "be")):
            mlp_rows[QUAD * m:QUAD * (m + 1), k] = g[f"{n}_{row}"]
    beta = np.zeros((ROWS, 3, D), f32)
    beta[BATCH:BATCH + KINDS, 0] = g["cp_b"]
    beta[BATCH:BATCH + KINDS, 1] = g["tm_b"]
    beta[BATCH + KINDS:, 2] = g["ms_b"]
    b1 = np.zeros((ROWS, D), f32)
    b1[0:BATCH] = g["int_b1"]
    arrays = {
        "x_in": a["x"].reshape(BATCH * SEQ, D),
        "sel_ids": sel,
        "idx_pw": by_tile(a["itok_BxS_0_999"]),
        "idx_kj": np.stack([by_tile(kinds), by_tile(scales)], 1),
        "pw_table": np.concatenate([g["pw_g"], g["pw_b"]], 1),
        "kj_table": np.concatenate([np.repeat(g["cp_g"], SCALES, 0), np.repeat(g["tm_g"], SCALES, 0),
                                    np.tile(g["ms_g"], (KINDS, 1))], 1),
        "mlp_x": mlp_x, "mlp_w1": mlp_w1,
        "mlp_w2": np.stack([g["mem_W2"], g["noi_W2"], g["res_W2"]]),
        "mlp_rows": mlp_rows, "beta_rows": beta, "b1_rows": b1,
        "int_w1": g["int_W1"], "int_w2": g["int_W2"], "b2_row": g["int_b2"].reshape(1, D),
        "norm_rows": np.stack([g["int_g"], g["int_be"], a["L1_cond_bias"]]),
        "aw": g["aw"],
        "weight_t": a["L1_cond_weight"].T, "affine_t": a["L1_cond_affine_w"].T,
        "affine_b": np.broadcast_to(a["L1_cond_affine_b"], (QUAD, D)),
        "eye": np.eye(P, dtype=f32), "sel_cmp": cmp,
    }
    arrays = {k: np.ascontiguousarray(v) for k, v in arrays.items()}
    nc = bacc.Bacc("TRN2", target_bir_lowering=False, num_devices=1)
    args = [nc.dram_tensor(k, v.shape, mybir.dt.from_np(v.dtype), kind="ExternalInput").ap() for k, v in arrays.items()]
    args.append(nc.dram_tensor("out", (BATCH * SEQ, D), F32, kind="ExternalOutput").ap())
    build(nc, *args)
    result = run_bass_kernel_spmd(nc, [arrays], core_ids=[0])
    return result.results[0]["out"].reshape(BATCH, SEQ, D)
```

```python
from contextlib import ExitStack

import concourse.bass as bass
from concourse import mybir

F32 = mybir.dt.float32
F32R = mybir.dt.float32r
BF16 = mybir.dt.bfloat16
I32 = mybir.dt.int32
ALU = mybir.AluOpType
ACT = mybir.ActivationFunctionType
AX = mybir.AxisListType

P = 128
D = 512
C = D // P
BATCH, SEQ = 8, 1024
TILES = BATCH * SEQ // P
PER_BATCH = SEQ // P
KINDS, SCALES = 5, 3
ROWS = BATCH + KINDS + SCALES
PARTS = 3
QUAD = 32
TROWS = PARTS * QUAD
EPS = 1e-5
DEMOD_EPS = 1e-8
CLAMP = 256.0
GAIN = 1.0 / 16.0
UNROLL = 2
FIRST = 4
LAST = TILES - 4


def build(nc, x, x_turned, sel, idx_pw, idx_kj, pw_table, kj_table, mlp_x, mlp_w1, mlp_w2, mlp_rows, beta_rows,
          int_w1, int_w2, norm_rows, aw, weight_t, affine_t, affine_b, eye, sel_cmp, out):
    with ExitStack() as ctx:
        def sb(name, shape, dt=F32):
            return ctx.enter_context(nc.sbuf_tensor(name, shape, dt))

        def sem(name):
            return ctx.enter_context(nc.semaphore(name))

        batch_rows_dram = nc.dram_tensor("batch_rows_dram", (BATCH, 2 * D), F32, kind="Internal").ap()

        wname = ("x", "t", "s", "h", "w2", "l1")
        w_hi = {n: sb(f"w_hi_{n}", [P, C, D], F32R) for n in wname}
        w_lo = {n: sb(f"w_lo_{n}", [P, C, D], F32R) for n in wname}
        norm_g = sb("norm_g", [P, 4, D])
        ident = sb("ident", [P, P])
        row_table = sb("row_table", [TROWS, D], BF16)
        cmp = sb("cmp", [TROWS, 1])
        pw_ids = sb("pw_ids", [P, TILES], I32)
        kj_ids = sb("kj_ids", [P, 2, TILES], I32)
        kj_index = sb("kj_index", [P, TILES], I32)
        half = sb("half", [P, 1])
        batch_rows = sb("batch_rows", [P, 2, 2 * D])

        work = sb("work", [P, 22 * D])
        place = [0]

        def carve(rows):
            a = place[0]
            place[0] += rows * D
            return work[:, a:a + rows * D].rearrange("p (n d) -> p n d", n=rows)

        gb, gk, z = [None, None], [None, None], [None, None]
        gb[0] = carve(2)
        gk[0] = carve(3)
        z[0] = carve(1)
        gk[1], z[1] = carve(3), carve(1)
        gb[1], xb = carve(2), carve(2)
        hid, vs = carve(1), carve(1)
        place[0] += 2 * D
        x1, yo = carve(2), carve(2)
        assert place[0] == 22 * D
        xt = sb("xt", [P, 2, D])
        xturn = sb("xturn", [P, 2, C, P])
        lhs_hi = {n: sb(f"lhs_hi_{n}", [P, C, P], F32R) for n in wname}
        lhs_lo = {n: sb(f"lhs_lo_{n}", [P, C, P], F32R) for n in wname}
        sel_in = sb("sel_in", [TROWS, 2, P], I32)
        onehot = sb("onehot", [TROWS, 2, P], BF16)
        ids_now = sb("ids_now", [P, 4], I32)
        raw = {n: sb(f"raw_{n}", [P, 2, 6]) for n in "xau"}
        mv = {n: sb(f"mv_{n}", [P, 2, 2]) for n in "xau"}
        ve = {n: sb(f"ve_{n}", [P, 2, 1]) for n in "xau"}
        rs = {n: sb(f"rs_{n}", [P, 2, 1]) for n in "xau"}

        stage = [work[:, (6 + 4 * k) * D:(10 + 4 * k) * D].rearrange("p (c d) -> p c d", c=4) for k in range(4)]
        aff_raw = stage[0][:, 0:2, :]
        affb = stage[0][0:QUAD, 2, :]
        mrows = stage[1][0:TROWS]
        mx = sb("mx", [P, 4, QUAD])
        mh = sb("mh", [TROWS, D])
        mhT = sb("mhT", [P, C, TROWS])
        rowT = sb("rowT", [P, 6, C, ROWS])
        beta = sb("beta", [QUAD, 4, D])
        style, dcoef = beta[:, 0, :], beta[:, 1, :]
        newton = beta[:, 2, :]
        b1r = beta[0:ROWS, 3, :]
        sqT = mhT[:, :, 0:QUAD]
        tableT = sb("tableT", [P, C, ROWS])
        soft = sb("soft", [P, 4, 8])
        wsm = soft[:, 3, 0:6]

        pre = ctx.enter_context(nc.psum_tensor("pre", [P, 2, D], F32))
        tb = ctx.enter_context(nc.psum_tensor("tb", [P, 4, D], F32))
        pu = ctx.enter_context(nc.psum_tensor("pu", [P, D], F32))
        py = ctx.enter_context(nc.psum_tensor("py", [P, D], F32))
        table_bank = (pre[:, 0, :], pre[:, 1, :], pu[:], py[:])

        ld = {n: sem(f"ld_{n}") for n in (
            "aw", "mx", "mw1", "mrows", "beta", "aff", "affb", "m0", "m1", "m2", "ident", "norm",
            "cmp", "ids", "l1", "w_m", "w_n", "w_r", "w_h", "w_t", "w_s", "w_w2")}
        aw_max, aw_exp, aw_ready = sem("aw_max"), sem("aw_exp"), sem("aw_ready")
        mlp1_mm, mlp1_add, mlp_h, h_tr, hT_ready = (sem(n) for n in ("mlp1_mm", "mlp1_add", "mlp_h", "h_tr", "hT_ready"))
        mlp2_mm, mlp2T_ready, mlp2_tr = sem("mlp2_mm"), sem("mlp2T_ready"), sem("mlp2_tr")
        c_var, c_rs, c_ready, c_tr, rowT_c = (sem(n) for n in ("c_var", "c_rs", "c_ready", "c_tr", "rowT_c"))
        styles_mm, styles_ready, styles_sq, sq_tr, sqT_ready = (
            sem(n) for n in ("styles_mm", "styles_ready", "styles_sq", "sq_tr", "sqT_ready"))
        wt_sq, dco_mm, dco_in, dco_root, dco_ready = (sem(n) for n in ("wt_sq", "dco_mm", "dco_in", "dco_root", "dco_ready"))
        style_stored, dcoef_stored = sem("style_stored"), sem("dcoef_stored")
        beta_tr, rowT_b = sem("beta_tr"), sem("rowT_b")
        table_mm = {n: sem(f"table_mm_{n}") for n in "htsmnr"}
        tableT_ready, table_tr, table_ready = sem("tableT_ready"), sem("table_tr"), sem("table_ready")
        hi_done = {n: sem(f"hi_done_{n}") for n in wname}
        lo_done = {n: sem(f"lo_done_{n}") for n in wname}
        wm_scaled, wn_added, wx_sum = sem("wm_scaled"), sem("wn_added"), sem("wx_sum")
        dve_step = sem("dve_step")
        half_set, kj_ready = sem("half_set"), sem("kj_ready")

        x_loaded = [sem(f"x_loaded_{u}") for u in range(2)]
        sel_loaded = [sem(f"sel_loaded_{u}") for u in range(2)]
        gb_loaded = [sem(f"gb_loaded_{u}") for u in range(2)]
        gk_loaded = [sem(f"gk_loaded_{u}") for u in range(2)]
        out_stored = [sem(f"out_stored_{u}") for u in range(2)]
        xturn_loaded = [sem(f"xturn_loaded_{u}") for u in range(2)]
        style_loaded, dcoef_loaded = sem("style_loaded"), sem("dcoef_loaded")
        ids_copied = sem("ids_copied")
        stats = {n: sem(f"stats_{n}") for n in "xau"}
        meanvar = {n: sem(f"meanvar_{n}") for n in "xau"}
        var_ready = {n: sem(f"var_ready_{n}") for n in "xau"}
        rstd_ready = {n: sem(f"rstd_ready_{n}") for n in "xau"}
        z_ready, zg_ready, a_ready, zh_ready = sem("z_ready"), sem("zg_ready"), sem("a_ready"), sem("zh_ready")
        t_ready, s_ready, h_ready = sem("t_ready"), sem("s_ready"), sem("h_ready")
        xb_ready, onehot_ready = sem("xb_ready"), sem("onehot_ready")
        turned = {n: sem(f"turned_{n}") for n in wname}
        hi_ready = {n: sem(f"hi_ready_{n}") for n in wname}
        lo_ready = {n: sem(f"lo_ready_{n}") for n in wname}
        mm_done = {n: sem(f"mm_done_{n}") for n in wname}
        hid_ready, u_ready, v_ready, x1_ready, x1s_ready = sem("hid_ready"), sem("u_ready"), sem("v_ready"), sem("x1_ready"), sem("x1s_ready")
        ys_ready, yb_ready, yc_ready, out_ready = sem("ys_ready"), sem("yb_ready"), sem("yc_ready"), sem("out_ready")

        def at_least(eng, s, n):
            if not isinstance(n, int) or n > 0:
                eng.wait_ge(s, n)

        def loaded(eng, sems, t, u):
            eng.wait_ge(sems[u], (t - u) * 8 + 16)

        def apart(eng):
            eng.wait_ge(ld["ident"], 16)

        def value(eng, n):
            return n if isinstance(n, int) else eng.to_reg(n)

        def batch_of(t):
            return t // PER_BATCH

        def batch_slot(t, what):
            b = batch_of(t) % 2
            if isinstance(t, int):
                return batch_rows[:, b, what * D:(what + 1) * D]
            return batch_rows[:].rearrange("p b d -> p (b d)")[:, bass.ds(b * (2 * D) + what * D, D)]

        def iterate(eng, body, between=None):
            for i in range(FIRST):
                body(i, i % 2)
                if i == 0 and between:
                    between()
            with eng.Fori(FIRST, LAST, UNROLL) as i:
                for k in range(UNROLL):
                    body(i + k, k)
            for i in range(LAST, TILES + 2):
                body(i, i % 2)

        def has(t):
            return not isinstance(t, int) or 0 <= t < TILES

        def w1_part(k):
            return int_w1[k * D:(k + 1) * D, :].rearrange("(c p) d -> p c d", p=P)

        block = ctx.enter_context(nc.Block())

        @block.sync
        def _(sp):
            def put(name, place, source):
                sp.dma_start(place, source).then_inc(ld[name], 16)

            def square(w):
                return w.rearrange("(c p) d -> p c d", p=P)

            put("aw", soft[:, 0, 0:6], aw.rearrange("(a k) -> a k", a=1).to_broadcast([P, 6]))
            put("ids", pw_ids[:], idx_pw)
            put("ids", kj_ids[:], idx_kj)
            put("mx", mx[:], mlp_x)
            put("mw1", stage[0], mlp_w1)
            put("mrows", mrows, mlp_rows)
            put("ident", ident[:], eye)
            put("beta", beta[:], beta_rows)
            put("cmp", cmp[:], sel_cmp)
            sp.dma_start(xt[:, 0, :], x[0:P, :]).then_inc(x_loaded[0], 16)
            sp.dma_start(sel_in[:, 0, :], sel[:, 0:P]).then_inc(sel_loaded[0], 16)
            put("m0", stage[2], square(mlp_w2[0]))
            sp.dma_start(xturn[:, 0, :, :], x_turned[:, 0:P].rearrange("(c p) t -> p c t", p=P)).then_inc(xturn_loaded[0], 16)
            put("m1", stage[3], square(mlp_w2[1]))
            sp.wait_ge(mlp1_mm, 1)
            put("m2", stage[0], square(mlp_w2[2]))
            sp.wait_ge(mlp2_mm, 1)
            put("w_h", stage[2], w1_part(0))
            sp.wait_ge(mlp2_mm, 2)
            put("w_t", stage[3], w1_part(1))
            sp.wait_ge(mlp2_mm, 3)
            put("aff", aff_raw, affine_t.rearrange("(c p) d -> p c d", p=P))
            put("affb", affb, affine_b)
            sp.wait_ge(c_ready, 1)
            put("w_m", stage[1], w1_part(2))
            sp.wait_ge(lo_done["h"], 1)
            sp.wait_ge(table_mm["h"], 1)
            put("w_s", stage[2], w1_part(5))
            sp.wait_ge(lo_done["t"], 1)
            sp.wait_ge(table_mm["t"], 1)
            put("w_n", stage[3], w1_part(3))
            put("norm", norm_g[:], norm_rows.rearrange("(a k) d -> a k d", a=1).to_broadcast([P, 4, D]))
            sp.wait_ge(lo_done["s"], 1)
            sp.wait_ge(table_mm["s"], 1)
            put("w_r", stage[2], w1_part(4))
            sp.wait_ge(wn_added, 1)
            sp.wait_ge(table_mm["n"], 1)
            put("l1", stage[3], square(weight_t))
            sp.wait_ge(styles_ready, 1)
            sp.dma_start(batch_rows_dram[:, 0:D], style[0:BATCH, :]).then_inc(style_stored, 16)
            sp.wait_ge(wx_sum, 1)
            sp.wait_ge(table_mm["r"], 1)
            put("w_w2", stage[2], square(int_w2))

            def load(t, u):
                apart(sp)
                at_least(sp, z_ready, t - 1)
                at_least(sp, xb_ready, t - 1)
                sp.dma_start(xt[:, u, :], x[bass.ds(t * P, P), :]).then_inc(x_loaded[u], 16)
                apart(sp)
                at_least(sp, onehot_ready, t - 1)
                sp.dma_start(sel_in[:, u, :], sel[:, bass.ds(t * P, P)]).then_inc(sel_loaded[u], 16)
                apart(sp)
                at_least(sp, lo_ready["x"], t - 1)
                sp.dma_start(xturn[:, u, :, :], x_turned[:, bass.ds(t * P, P)].rearrange("(c p) t -> p c t", p=P)).then_inc(xturn_loaded[u], 16)

            def load_row(b, what, used, arrived):
                apart(sp)
                at_least(sp, used, (b - 1) * PER_BATCH)
                if isinstance(b, int):
                    place = batch_rows[:, b % 2, what * D:(what + 1) * D]
                else:
                    place = batch_rows[:].rearrange("p b d -> p (b d)")[:, bass.ds((b % 2) * (2 * D) + what * D, D)]
                row = batch_rows_dram[bass.ds(b, 1), what * D:(what + 1) * D]
                sp.dma_start(place, row.to_broadcast([P, D])).then_inc(arrived, 16)

            def load_rows(b):
                load_row(b, 0, x1s_ready, style_loaded)
                load_row(b, 1, ys_ready, dcoef_loaded)

            def store(t, u):
                apart(sp)
                sp.wait_ge(out_ready, t + 1)
                sp.dma_start(out[bass.ds(t * P, P), :], yo[:, u, :]).then_inc(out_stored[u], 16)

            load(1, 1)
            sp.wait_ge(style_stored, 16)
            load_row(0, 0, x1s_ready, style_loaded)

            def step(i, u):
                if has(i + 2):
                    load(i + 2, u)
                if has(i - 2):
                    store(i - 2, u)

            for i in range(PER_BATCH):
                if i == 2:
                    sp.wait_ge(dco_ready, 1)
                    sp.dma_start(batch_rows_dram[:, D:2 * D], dcoef[0:BATCH, :]).then_inc(dcoef_stored, 16)
                    sp.wait_ge(dcoef_stored, 16)
                    load_row(0, 1, ys_ready, dcoef_loaded)
                step(i, i % 2)
            with sp.Fori(1, BATCH - 1) as b:
                load_rows(b)
                with sp.Fori(0, PER_BATCH, UNROLL) as k:
                    for u in range(UNROLL):
                        step(b * PER_BATCH + k + u, u)
            load_rows(BATCH - 1)
            for i in range(TILES - PER_BATCH, TILES + 2):
                step(i, i % 2)
            for u in range(2):
                sp.wait_ge(out_stored[u], 8 * TILES)

        @block.gpsimd
        def _(pool):
            nc.gpsimd.memset(half[:], -0.5).then_inc(half_set, 1)
            pool.wait_ge(half_set, 1)
            pool.wait_ge(kj_ready, 1)
            pool.wait_ge(ld["ids"], 32)

            def gather(t, u):
                at_least(pool, h_ready, t - 1)
                at_least(pool, turned["h"], t - 1)
                count = value(pool, 2 * t + 2)
                nc.gpsimd.tensor_copy(ids_now[:, u:u + 1], pw_ids[:, bass.ds(t, 1)]).then_inc(ids_copied, 1)
                nc.gpsimd.tensor_copy(ids_now[:, 2 + u:3 + u], kj_index[:, bass.ds(t, 1)]).then_inc(ids_copied, 1)
                apart(pool)
                pool.wait_ge(ids_copied, count)
                pool.indirect_dma_start(gb[u].rearrange("p n d -> p (n d)"), None, pw_table,
                                        bass.IndirectOffsetOnAxis(ids_now[:, u:u + 1], 0)).then_inc(gb_loaded[u], 16)
                pool.indirect_dma_start(gk[u].rearrange("p n d -> p (n d)"), None, kj_table,
                                        bass.IndirectOffsetOnAxis(ids_now[:, 2 + u:3 + u], 0)).then_inc(gk_loaded[u], 16)

            def rstd(n, t, u):
                pool.wait_ge(var_ready[n], t + 1)
                nc.gpsimd.tensor_tensor(rs[n][:, u, :], ve[n][:, u, :], half[:], ALU.pow).then_inc(rstd_ready[n], 1)

            def ahead(f, v):
                rstd("x", f, v)
                pool.wait_ge(z_ready, f + 1)
                loaded(pool, gb_loaded, f, v)
                nc.gpsimd.tensor_tensor(gb[v][:, 0, :], z[v][:, 0, :], gb[v][:, 0, :], ALU.mult).then_inc(zg_ready, 1)
                pool.wait_ge(zg_ready, f + 1)
                nc.gpsimd.tensor_tensor(gb[v][:, 0, :], gb[v][:, 0, :], gb[v][:, 1, :], ALU.add).then_inc(a_ready, 1)
                rstd("a", f, v)

            def add_be(f, v):
                loaded(pool, x_loaded, f, v)
                at_least(pool, x1_ready, f - 1)
                nc.gpsimd.tensor_tensor(xb[:, v, :], xt[:, v, :], norm_g[:, 1, :], ALU.add).then_inc(xb_ready, 1)

            gather(0, 0)
            ahead(0, 0)
            pool.wait_ge(c_var, 1)
            nc.gpsimd.tensor_tensor(rs["u"][0:TROWS, 0, :], ve["u"][0:TROWS, 0, :], half[0:TROWS, :], ALU.pow).then_inc(c_rs, 1)
            pool.wait_ge(lo_done["x"], 1)
            pool.wait_ge(styles_ready, 1)
            gather(1, 1)
            pool.wait_ge(ld["norm"], 16)
            add_be(0, 0)
            pool.wait_ge(hi_done["w2"], 1)
            nc.gpsimd.tensor_tensor(w_lo["w2"][:], stage[2], w_hi["w2"][:].bitcast(F32), ALU.subtract).then_inc(lo_done["w2"], 1)

            def body(i, u):
                f, v = i + 1, 1 - u
                if has(f):
                    ahead(f, v)
                if has(i + 2):
                    gather(i + 2, u)
                if has(i - 1):
                    rstd("u", i - 1, v)
                if has(i - 2):
                    t = i - 2
                    pool.wait_ge(ys_ready, t + 1)
                    nc.gpsimd.tensor_tensor(yo[:, u, :], yo[:, u, :], norm_g[:, 2, :], ALU.add).then_inc(yb_ready, 1)
                    apart(pool)
                    pool.wait_ge(yb_ready, t + 1)
                    nc.gpsimd.tensor_scalar(yo[:, u, :], yo[:, u, :], CLAMP, -CLAMP, ALU.min, ALU.max).then_inc(yc_ready, 1)
                    pool.wait_ge(yc_ready, t + 1)
                    nc.gpsimd.tensor_tensor(yo[:, u, :], yo[:, u, :], x1[:, u, :], ALU.add).then_inc(out_ready, 1)
                if has(i - 1):
                    t = i - 1
                    pool.wait_ge(x1_ready, t + 1)
                    pool.wait_ge(style_loaded, batch_of(t) * 16 + 16)
                    nc.gpsimd.tensor_tensor(vs[:, 0, :], x1[:, v, :], batch_slot(t, 0), ALU.mult).then_inc(x1s_ready, 1)
                if has(f):
                    add_be(f, v)

            iterate(pool, body)

        @block.scalar
        def _(act):
            act.wait_ge(aw_max, 1)
            nc.scalar.activation(soft[:, 1, 0:6], soft[:, 0, 0:6], ACT.Exp, bias=soft[:, 2, 0:1]).then_inc(aw_exp, 1)
            act.wait_ge(mlp1_add, 1)
            nc.scalar.activation(mh[:], mh[:], ACT.Silu).then_inc(mlp_h, 1)

            def high(n, k, scale=None):
                nc.scalar.activation(w_hi[n][:], stage[k], ACT.Copy, scale=1.0 if scale is None else scale).then_inc(hi_done[n], 1)

            def split(n, bank, t):
                act.wait_ge(turned[n], t + 1)
                at_least(act, mm_done[n], t)
                nc.scalar.activation(lhs_hi[n][:].rearrange("p c t -> p (c t)"), tb[:, bank, :], ACT.Copy).then_inc(hi_ready[n], 1)

            def split_x(t, u):
                loaded(act, xturn_loaded, t, u)
                at_least(act, mm_done["x"], t)
                nc.scalar.activation(lhs_hi["x"][:], xturn[:, u, :, :], ACT.Copy).then_inc(hi_ready["x"], 1)

            split_x(0, 0)
            split("t", 1, 0)
            act.wait_ge(aw_ready, 1)
            act.wait_ge(ld["w_h"], 16)
            high("h", 2, wsm[:, 0:1])
            act.wait_ge(ld["w_t"], 16)
            high("t", 3, wsm[:, 1:2])
            act.wait_ge(ld["w_s"], 16)
            high("s", 2, wsm[:, 5:6])
            act.wait_ge(ld["w_m"], 16)
            act.wait_ge(table_mm["m"], 1)
            nc.scalar.activation(stage[1], stage[1], ACT.Copy, scale=wsm[:, 2:3]).then_inc(wm_scaled, 1)
            act.wait_ge(wx_sum, 1)
            high("x", 1)
            act.wait_ge(ld["l1"], 16)
            high("l1", 3)
            act.wait_ge(ld["w_w2"], 16)
            high("w2", 2)
            act.wait_ge(lo_done["l1"], 1)
            nc.scalar.activation(stage[3], stage[3], ACT.Square).then_inc(wt_sq, 1)

            def root():
                act.wait_ge(dco_in, 1)
                nc.scalar.activation(newton, dcoef, ACT.Sqrt).then_inc(dco_root, 1)

            def body(i, u):
                if has(i - 1):
                    split("w2", 0, i - 1)
                if has(i):
                    split("s", 1, i)
                if has(i - 2):
                    split("l1", 2, i - 2)
                if has(i):
                    split("h", 3, i)
                if has(i + 1):
                    split_x(i + 1, 1 - u)
                    split("t", 1, i + 1)
                if has(i):
                    act.wait_ge(mm_done["h"], i + 1)
                    at_least(act, turned["w2"], i)
                    if isinstance(i, int) and i == 0:
                        act.wait_ge(lo_done["w2"], 1)
                    nc.scalar.activation(hid[:, 0, :], pre[:, u, :], ACT.Silu).then_inc(hid_ready, 1)

            iterate(act, body, root)

        @block.vector
        def _(dve):
            steps = [0]

            def link(ins):
                steps[0] += 1
                ins.then_inc(dve_step, 1)
                dve.wait_ge(dve_step, steps[0])

            dve.wait_ge(ld["aw"], 16)
            link(nc.vector.tensor_reduce(soft[:, 2, 1:2], soft[:, 0, 0:6], AX.X, ALU.max))
            nc.vector.tensor_scalar(soft[:, 2, 0:1], soft[:, 2, 1:2], -1.0, None, ALU.mult).then_inc(aw_max, 1)
            dve.wait_ge(aw_exp, 1)
            link(nc.vector.tensor_reduce(soft[:, 2, 2:3], soft[:, 1, 0:6], AX.X, ALU.add))
            link(nc.vector.reciprocal(soft[:, 2, 3:4], soft[:, 2, 2:3]))
            nc.vector.tensor_scalar(wsm, soft[:, 1, 0:6], soft[:, 2, 3:4], None, ALU.mult).then_inc(aw_ready, 1)
            dve.wait_ge(ld["ids"], 32)
            nc.vector.scalar_tensor_tensor(out=kj_index[:], in0=kj_ids[:, 0, :], scalar=float(SCALES), in1=kj_ids[:, 1, :],
                                           op0=ALU.mult, op1=ALU.add).then_inc(kj_ready, 1)
            nc.vector.memset(row_table[:], 0.0)
            link(nc.vector.memset(rowT[:], 0.0))
            dve.wait_ge(mlp1_mm, 1)
            dve.wait_ge(ld["mrows"], 16)
            nc.vector.tensor_tensor(mh[:], tb[0:TROWS, 3, :], mrows[:, 0, :], ALU.add).then_inc(mlp1_add, 1)
            dve.wait_ge(beta_tr, 1)
            dve.wait_ge(aw_ready, 1)
            for k, unit in enumerate((0, 1, 5)):
                src = tb[:, 2, k * C * ROWS:(k + 1) * C * ROWS].rearrange("p (c r) -> p c r", c=C)
                nc.vector.tensor_scalar(rowT[:, unit, :, :], src, wsm[:, unit:unit + 1], None, ALU.mult).then_inc(rowT_b, 1)
            dve.wait_ge(h_tr, 1)
            nc.vector.tensor_copy(mhT[:].rearrange("p c r -> p (c r)"), tb[:, 0, 0:C * TROWS]).then_inc(hT_ready, 1)

            def moments(n, src, t, u):
                count = value(dve, t + 1)
                nc.vector.bn_stats(raw[n][:, u, :], src).then_inc(stats[n], 1)
                apart(dve)
                dve.wait_ge(stats[n], count)
                nc.vector.bn_aggr(mv[n][:, u, :], raw[n][:, u, :]).then_inc(meanvar[n], 1)
                dve.wait_ge(meanvar[n], t + 1)
                nc.vector.tensor_scalar(ve[n][:, u, :], mv[n][:, u, 1:2], EPS, None, ALU.add).then_inc(var_ready[n], 1)

            def low_part(n, bank, t):
                dve.wait_ge(hi_ready[n], t + 1)
                nc.vector.tensor_tensor(lhs_lo[n][:].rearrange("p c t -> p (c t)"), tb[:, bank, :],
                                        lhs_hi[n][:].rearrange("p c t -> p (c t)").bitcast(F32), ALU.subtract).then_inc(lo_ready[n], 1)

            def low_x(t, u):
                dve.wait_ge(hi_ready["x"], t + 1)
                nc.vector.tensor_tensor(lhs_lo["x"][:], xturn[:, u, :, :], lhs_hi["x"][:].bitcast(F32), ALU.subtract).then_inc(lo_ready["x"], 1)

            def normal(f, v):
                dve.wait_ge(rstd_ready["x"], f + 1)
                at_least(dve, zg_ready, f - 1)
                at_least(dve, s_ready, f - 1)
                nc.vector.tensor_scalar(z[v][:, 0, :], xt[:, v, :], mv["x"][:, v, 0:1], rs["x"][:, v, :],
                                        ALU.subtract, ALU.mult).then_inc(z_ready, 1)

            def gated(f, v):
                dve.wait_ge(z_ready, f + 1)
                loaded(dve, gk_loaded, f, v)
                nc.vector.tensor_tensor(gk[v][:, 1, :], z[v][:, 0, :], gk[v][:, 1, :], ALU.mult).then_inc(t_ready, 1)
                nc.vector.tensor_tensor(gk[v][:, 2, :], z[v][:, 0, :], gk[v][:, 2, :], ALU.mult).then_inc(s_ready, 1)
                loaded(dve, sel_loaded, f, v)
                at_least(dve, mm_done["h"], f - 1)
                nc.vector.tensor_scalar(onehot[:, v, :], sel_in[:, v, :], cmp[:, 0:1], None, ALU.is_equal).then_inc(onehot_ready, 1)

            def second_normal(f, v):
                dve.wait_ge(rstd_ready["a"], f + 1)
                nc.vector.tensor_scalar(gb[v][:, 0, :], gb[v][:, 0, :], mv["a"][:, v, 0:1], rs["a"][:, v, :],
                                        ALU.subtract, ALU.mult).then_inc(zh_ready, 1)
                dve.wait_ge(zh_ready, f + 1)
                nc.vector.tensor_tensor(gk[v][:, 0, :], gb[v][:, 0, :], gk[v][:, 0, :], ALU.mult).then_inc(h_ready, 1)

            loaded(dve, x_loaded, 0, 0)
            moments("x", xt[:, 0, :], 0, 0)
            normal(0, 0)
            dve.wait_ge(ld["cmp"], 16)
            gated(0, 0)
            low_x(0, 0)
            dve.wait_ge(a_ready, 1)
            moments("a", gb[0][:, 0, :], 0, 0)
            second_normal(0, 0)
            low_part("t", 1, 0)

            dve.wait_ge(mlp2_mm, 3)
            nc.vector.tensor_copy(mhT[:].rearrange("p c r -> p (c r)"), tb[:, 3, 0:C * TROWS]).then_inc(mlp2T_ready, 1)
            dve.wait_ge(mlp2_tr, 1)
            link(nc.vector.tensor_tensor(mh[:], tb[0:TROWS, 0, :], mrows[:, 1, :], ALU.add))
            link(nc.vector.bn_stats(raw["u"][0:TROWS, 0, :], mh[:]))
            link(nc.vector.bn_aggr(mv["u"][0:TROWS, 0, :], raw["u"][0:TROWS, 0, :]))
            nc.vector.tensor_scalar(ve["u"][0:TROWS, 0, :], mv["u"][0:TROWS, 0, 1:2], EPS, None, ALU.add).then_inc(c_var, 1)
            dve.wait_ge(c_rs, 1)
            link(nc.vector.tensor_scalar(mh[:], mh[:], mv["u"][0:TROWS, 0, 0:1], rs["u"][0:TROWS, 0, :], ALU.subtract, ALU.mult))
            link(nc.vector.tensor_tensor(mh[:], mh[:], mrows[:, 2, :], ALU.mult))
            nc.vector.tensor_tensor(mh[:], mh[:], mrows[:, 3, :], ALU.add).then_inc(c_ready, 1)

            flat = "p c d -> p (c d)"

            def low(n, k, scale):
                dve.wait_ge(hi_done[n], 1)
                nc.vector.scalar_tensor_tensor(out=w_lo[n][:].rearrange(flat), in0=stage[k].rearrange(flat), scalar=scale,
                                               in1=w_hi[n][:].bitcast(F32).rearrange(flat), op0=ALU.mult, op1=ALU.subtract).then_inc(lo_done[n], 1)

            low("h", 2, wsm[:, 0:1])
            dve.wait_ge(c_tr, 1)
            for m in range(3):
                src = tb[:, 3, 0:C * TROWS].rearrange("p (c r) -> p c r", c=C)[:, :, QUAD * m:QUAD * m + BATCH]
                nc.vector.tensor_scalar(rowT[:, 2 + m, :, 0:BATCH], src, wsm[:, 2 + m:3 + m], None, ALU.mult).then_inc(rowT_c, 1)
            low("t", 3, wsm[:, 1:2])
            dve.wait_ge(styles_mm, 1)
            dve.wait_ge(ld["affb"], 16)
            nc.vector.scalar_tensor_tensor(out=style, in0=tb[0:QUAD, 2, :], scalar=GAIN, in1=affb,
                                           op0=ALU.mult, op1=ALU.add).then_inc(styles_ready, 1)
            dve.wait_ge(styles_ready, 1)
            nc.vector.tensor_tensor(dcoef, style, style, ALU.mult).then_inc(styles_sq, 1)
            dve.wait_ge(sq_tr, 1)
            nc.vector.tensor_copy(sqT, tb[:, 0, 0:C * QUAD].rearrange("p (c r) -> p c r", c=C)).then_inc(sqT_ready, 1)
            low("s", 2, wsm[:, 5:6])
            for n, k, w, done in (("w_n", 3, 3, wn_added), ("w_r", 2, 4, wx_sum)):
                dve.wait_ge(ld[n], 16)
                dve.wait_ge(wm_scaled, 1)
                nc.vector.scalar_tensor_tensor(out=stage[1].rearrange(flat), in0=stage[k].rearrange(flat), scalar=wsm[:, w:w + 1],
                                               in1=stage[1].rearrange(flat), op0=ALU.mult, op1=ALU.add).then_inc(done, 1)
                dve.wait_ge(done, 1)
            low("x", 1, 1.0)
            dve.wait_ge(table_mm["r"], 1)
            for c in range(C):
                nc.vector.tensor_copy(tableT[:, c, :], table_bank[c][:, 0:ROWS]).then_inc(tableT_ready, 1)
            dve.wait_ge(table_tr, 1)
            link(nc.vector.tensor_tensor(b1r, tb[0:ROWS, 2, :], b1r, ALU.add))
            for k in range(PARTS):
                part = row_table[QUAD * k:QUAD * k + ROWS, :]
                if k + 1 == PARTS:
                    nc.vector.tensor_copy(part, b1r).then_inc(table_ready, 1)
                else:
                    link(nc.vector.tensor_copy(part, b1r))
                    link(nc.vector.tensor_copy(mh[0:ROWS, :], part))
                    link(nc.vector.tensor_tensor(b1r, b1r, mh[0:ROWS, :], ALU.subtract))
            low("l1", 3, 1.0)
            dve.wait_ge(ld["norm"], 16)

            def demod_in():
                dve.wait_ge(dco_mm, 1)
                nc.vector.tensor_scalar(dcoef, py[0:QUAD, :], DEMOD_EPS, None, ALU.add).then_inc(dco_in, 1)

            def demod_out():
                dve.wait_ge(dco_root, 1)
                r, q = newton, mh[0:QUAD, :]
                link(nc.vector.reciprocal(r, r))
                link(nc.vector.tensor_tensor(q, r, r, ALU.mult))
                link(nc.vector.tensor_tensor(q, q, dcoef, ALU.mult))
                link(nc.vector.tensor_scalar(q, q, -0.5, 1.5, ALU.mult, ALU.add))
                nc.vector.tensor_tensor(dcoef, q, r, ALU.mult).then_inc(dco_ready, 1)

            def body(i, u):
                f, v = i + 1, 1 - u
                if has(f):
                    loaded(dve, x_loaded, f, v)
                    moments("x", xt[:, v, :], f, v)
                if has(i - 1):
                    low_part("w2", 0, i - 1)
                if has(f):
                    normal(f, v)
                if has(i):
                    low_part("s", 1, i)
                if has(f):
                    gated(f, v)
                if has(i - 2):
                    low_part("l1", 2, i - 2)
                if has(i):
                    low_part("h", 3, i)
                if isinstance(i, int) and i == 1:
                    demod_out()
                if has(f):
                    dve.wait_ge(a_ready, f + 1)
                    moments("a", gb[v][:, 0, :], f, v)
                if has(i - 1):
                    t = i - 1
                    dve.wait_ge(mm_done["w2"], t + 1)
                    at_least(dve, turned["l1"], t)
                    nc.vector.tensor_tensor(vs[:, 0, :], pu[:], norm_g[:, 3, :], ALU.add).then_inc(u_ready, 1)
                    dve.wait_ge(u_ready, t + 1)
                    moments("u", vs[:, 0, :], t, v)
                if has(f):
                    second_normal(f, v)
                if has(i - 1):
                    nc.vector.scalar_tensor_tensor(out=vs[:, 0, :], in0=vs[:, 0, :], scalar=mv["u"][:, v, 0:1], in1=norm_g[:, 0, :],
                                                   op0=ALU.subtract, op1=ALU.mult).then_inc(v_ready, 1)
                    dve.wait_ge(rstd_ready["u"], t + 1)
                    dve.wait_ge(v_ready, t + 1)
                    dve.wait_ge(xb_ready, t + 1)
                    at_least(dve, out_ready, t - 1)
                    nc.vector.scalar_tensor_tensor(out=x1[:, v, :], in0=vs[:, 0, :], scalar=rs["u"][:, v, :], in1=xb[:, v, :],
                                                   op0=ALU.mult, op1=ALU.add).then_inc(x1_ready, 1)
                if has(i - 2):
                    t = i - 2
                    dve.wait_ge(mm_done["l1"], t + 1)
                    dve.wait_ge(dcoef_loaded, batch_of(t) * 16 + 16)
                    if not isinstance(t, int) or t >= 2:
                        loaded(dve, out_stored, t - 2, u)
                    nc.vector.tensor_tensor(yo[:, u, :], py[:], batch_slot(t, 1), ALU.mult).then_inc(ys_ready, 1)
                if has(f):
                    low_x(f, v)
                    low_part("t", 1, f)

            iterate(dve, body, demod_in)

        @block.tensor
        def _(pe):
            for n in ("mx", "mw1"):
                pe.wait_ge(ld[n], 16)
            for m, chunks in enumerate(((0, 1), (2,), (3,))):
                for c in chunks:
                    last = pe.matmul(tb[QUAD * m:QUAD * (m + 1), 3, :], mx[:, c, :], stage[0][:, c, :],
                                     start=c == chunks[0], stop=c == chunks[-1])
            last.then_inc(mlp1_mm, 1)
            pe.wait_ge(ld["ident"], 16)
            pe.wait_ge(ld["beta"], 16)
            for k in range(3):
                for c in range(C):
                    at = (k * C + c) * ROWS
                    last = pe.transpose(tb[:, 2, at:at + ROWS], beta[0:ROWS, k, c * P:(c + 1) * P], ident[0:ROWS, 0:ROWS])
            last.then_inc(beta_tr, 1)
            pe.wait_ge(mlp_h, 1)
            for c in range(C):
                last = pe.transpose(tb[:, 0, c * TROWS:(c + 1) * TROWS], mh[:, c * P:(c + 1) * P], ident[0:TROWS, 0:TROWS])
            last.then_inc(h_tr, 1)

            def turn(n, bank, src):
                for c in range(C):
                    last = pe.transpose(tb[:, bank, c * P:(c + 1) * P], src[:, c * P:(c + 1) * P], ident[:])
                last.then_inc(turned[n], 1)

            pe.wait_ge(hT_ready, 1)
            for m, k in enumerate((2, 3, 0)):
                pe.wait_ge(ld[f"m{m}"], 16)
                for o in range(C):
                    at = o * TROWS + QUAD * m
                    for c in range(C):
                        last = pe.matmul(tb[:, 3, at:at + QUAD], stage[k][:, c, o * P:(o + 1) * P],
                                         mhT[:, c, QUAD * m:QUAD * (m + 1)], start=c == 0, stop=c == C - 1)
                last.then_inc(mlp2_mm, 1)
                if m == 1:
                    pe.wait_ge(t_ready, 1)
                    turn("t", 1, gk[0][:, 1, :])

            def table(n, unit, k, first=False, last_one=False):
                pe.wait_ge(ld[f"w_{n}"], 16)
                for c in range(C):
                    for o in range(C):
                        last = pe.matmul(table_bank[o][:, 0:ROWS], stage[k][:, c, o * P:(o + 1) * P], rowT[:, unit, c, :],
                                         start=first and c == 0, stop=last_one and c == C - 1)
                last.then_inc(table_mm[n], 1)

            def back(bank, src, rows, s):
                for c in range(C):
                    last = pe.transpose(tb[0:rows, bank, c * P:(c + 1) * P], src[:, c, :], ident[:])
                last.then_inc(s, 1)

            pe.wait_ge(mlp2T_ready, 1)
            back(0, mhT, TROWS, mlp2_tr)
            pe.wait_ge(rowT_b, 3)
            table("h", 0, 2, first=True)
            pe.wait_ge(c_ready, 1)
            for c in range(C):
                last = pe.transpose(tb[:, 3, c * TROWS:(c + 1) * TROWS], mh[:, c * P:(c + 1) * P], ident[0:TROWS, 0:TROWS])
            last.then_inc(c_tr, 1)
            table("t", 1, 3)
            pe.wait_ge(ld["aff"], 16)
            for c in range(2):
                last = pe.matmul(tb[0:QUAD, 2, :], mx[:, c, :], aff_raw[:, c, :], start=c == 0, stop=c == 1)
            last.then_inc(styles_mm, 1)
            pe.wait_ge(styles_sq, 1)
            for c in range(C):
                last = pe.transpose(tb[:, 0, c * QUAD:(c + 1) * QUAD], dcoef[:, c * P:(c + 1) * P], ident[0:QUAD, 0:QUAD])
            last.then_inc(sq_tr, 1)
            table("s", 5, 2)
            pe.wait_ge(rowT_c, 3)
            table("m", 2, 1)
            table("n", 3, 3)
            table("r", 4, 2, last_one=True)
            pe.wait_ge(tableT_ready, C)
            back(2, tableT, ROWS, table_tr)

            def demod():
                pe.wait_ge(sqT_ready, 1)
                pe.wait_ge(wt_sq, 1)
                for c in range(C):
                    last = pe.matmul(py[0:QUAD, :], sqT[:, c, :], stage[3][:, c, :], start=c == 0, stop=c == C - 1)
                last.then_inc(dco_mm, 1)

            def unit(n, t, dst, start, stop):
                if isinstance(t, int) and t == 0:
                    pe.wait_ge(lo_done[n], 1)
                passes = ((lhs_hi, w_hi), (lhs_hi, w_lo), (lhs_lo, w_hi))
                for c in range(C):
                    for k, (a, b) in enumerate(passes):
                        last = pe.matmul(dst, a[n][:, c, :], b[n][:, c, :], start=start and c == 0 and k == 0,
                                         stop=stop and c == C - 1 and k == 2)
                last.then_inc(mm_done[n], 1)

            def body(i, u):
                v = 1 - u
                if has(i):
                    at_least(pe, hid_ready, i - 1)
                    pe.wait_ge(lo_ready["x"], i + 1)
                    unit("x", i, pre[:, u, :], True, False)
                if has(i - 1):
                    pe.wait_ge(hid_ready, i)
                    turn("w2", 0, hid[:, 0, :])
                if has(i):
                    pe.wait_ge(s_ready, i + 1)
                    pe.wait_ge(lo_ready["t"], i + 1)
                    turn("s", 1, gk[u][:, 2, :])
                    unit("t", i, pre[:, u, :], False, False)
                if has(i - 2):
                    pe.wait_ge(x1s_ready, i - 1)
                    at_least(pe, lo_ready["l1"], i - 2)
                    turn("l1", 2, vs[:, 0, :])
                if has(i):
                    pe.wait_ge(h_ready, i + 1)
                    at_least(pe, lo_ready["h"], i)
                    turn("h", 3, gk[u][:, 0, :])
                if has(i - 1):
                    pe.wait_ge(lo_ready["w2"], i)
                    at_least(pe, u_ready, i - 1)
                    unit("w2", i - 1, pu[:], True, True)
                if has(i - 2):
                    pe.wait_ge(lo_ready["l1"], i - 1)
                    if isinstance(i, int) and i == 2:
                        pe.wait_ge(dco_in, 1)
                    at_least(pe, ys_ready, i - 2)
                    unit("l1", i - 2, py[:], True, True)
                if has(i):
                    pe.wait_ge(lo_ready["s"], i + 1)
                    unit("s", i, pre[:, u, :], False, False)
                if has(i + 1):
                    pe.wait_ge(t_ready, i + 2)
                    turn("t", 1, gk[v][:, 1, :])
                if has(i):
                    pe.wait_ge(onehot_ready, i + 1)
                    if isinstance(i, int) and i == 0:
                        pe.wait_ge(table_ready, 1)
                    pe.matmul(pre[:, u, :], onehot[:, u, :], row_table[:], start=False, stop=False)
                    pe.wait_ge(lo_ready["h"], i + 1)
                    unit("h", i, pre[:, u, :], False, True)

            iterate(pe, body, demod)


def kernel(**inputs):
    import numpy as np
    import concourse.bacc as bacc
    from concourse.bass_utils import run_bass_kernel_spmd

    a = {k: np.asarray(v) for k, v in inputs.items()}
    g = {k[len("L0_cond_"):]: v for k, v in a.items() if k.startswith("L0_cond_")}
    f32 = np.float32

    def by_tile(ids):
        return ids.reshape(TILES, P).T

    kinds, scales = a["itok_BxS_0_4"], a["mask_BxS_ik0"]
    sel = np.full((TROWS, BATCH * SEQ), -1, np.int32)
    cmp = np.zeros((TROWS, 1), f32)
    for k in range(PARTS):
        r = QUAD * k
        sel[r:r + BATCH] = np.repeat(np.arange(BATCH, dtype=np.int32), SEQ)
        sel[r + BATCH:r + BATCH + KINDS] = kinds.reshape(-1)
        sel[r + BATCH + KINDS:r + ROWS] = scales.reshape(-1)
        cmp[r:r + ROWS, 0] = [*range(BATCH), *range(KINDS), *range(SCALES)]
    mlp_x = np.zeros((P, 4, QUAD), f32)
    mlp_x[:, 0:2, 0:BATCH] = a["cond_512"].T.reshape(2, P, BATCH).transpose(1, 0, 2)
    mlp_x[0:64, 2, 0:BATCH] = a["cond_64"].T
    mlp_x[0:32, 3, 0:BATCH] = a["fside_Bx32_0"].T
    mlp_w1 = np.zeros((P, 4, D), f32)
    mlp_w1[:, 0:2] = g["mem_W1"].reshape(2, P, D).transpose(1, 0, 2)
    mlp_w1[0:64, 2] = g["noi_W1"]
    mlp_w1[0:32, 3] = g["res_W1"]
    mlp_rows = np.zeros((TROWS, 4, D), f32)
    for m, n in enumerate(("mem", "noi", "res")):
        for k, row in enumerate(("b1", "b2", "g", "be")):
            mlp_rows[QUAD * m:QUAD * (m + 1), k] = g[f"{n}_{row}"]
    beta = np.zeros((QUAD, 4, D), f32)
    beta[BATCH:BATCH + KINDS, 0] = g["cp_b"]
    beta[BATCH:BATCH + KINDS, 1] = g["tm_b"]
    beta[BATCH + KINDS:ROWS, 2] = g["ms_b"]
    beta[0:BATCH, 3] = g["int_b1"]
    arrays = {
        "x_in": a["x"].reshape(BATCH * SEQ, D),
        "x_turned": a["x"].reshape(BATCH * SEQ, D).T,
        "sel_ids": sel,
        "idx_pw": by_tile(a["itok_BxS_0_999"]),
        "idx_kj": np.stack([by_tile(kinds), by_tile(scales)], 1),
        "pw_table": np.concatenate([g["pw_g"], g["pw_b"]], 1),
        "kj_table": np.concatenate([np.repeat(g["cp_g"], SCALES, 0), np.repeat(g["tm_g"], SCALES, 0),
                                    np.tile(g["ms_g"], (KINDS, 1))], 1),
        "mlp_x": mlp_x, "mlp_w1": mlp_w1,
        "mlp_w2": np.stack([g["mem_W2"], g["noi_W2"], g["res_W2"]]),
        "mlp_rows": mlp_rows, "beta_rows": beta,
        "int_w1": g["int_W1"], "int_w2": g["int_W2"],
        "norm_rows": np.stack([g["int_g"], g["int_be"], a["L1_cond_bias"], g["int_b2"]]),
        "aw": g["aw"],
        "weight_t": a["L1_cond_weight"].T, "affine_t": a["L1_cond_affine_w"].T,
        "affine_b": np.broadcast_to(a["L1_cond_affine_b"], (QUAD, D)),
        "eye": np.eye(P, dtype=f32), "sel_cmp": cmp,
    }
    arrays = {k: np.ascontiguousarray(v) for k, v in arrays.items()}
    nc = bacc.Bacc("TRN2", target_bir_lowering=False, num_devices=1)
    args = [nc.dram_tensor(k, v.shape, mybir.dt.from_np(v.dtype), kind="ExternalInput").ap() for k, v in arrays.items()]
    args.append(nc.dram_tensor("out", (BATCH * SEQ, D), F32, kind="ExternalOutput").ap())
    build(nc, *args)
    result = run_bass_kernel_spmd(nc, [arrays], core_ids=[0])
    return result.results[0]["out"].reshape(BATCH, SEQ, D)
```

```python
from contextlib import ExitStack

import concourse.bass as bass
from concourse import mybir

F32 = mybir.dt.float32
F32R = mybir.dt.float32r
BF16 = mybir.dt.bfloat16
I32 = mybir.dt.int32
ALU = mybir.AluOpType
ACT = mybir.ActivationFunctionType
AX = mybir.AxisListType

P = 128
D = 512
C = D // P
BATCH, SEQ = 8, 1024
TILES = BATCH * SEQ // P
PER_BATCH = SEQ // P
KINDS, SCALES = 5, 3
ROWS = BATCH + KINDS + SCALES
PARTS = 3
QUAD = 32
TROWS = PARTS * QUAD
EPS = 1e-5
DEMOD_EPS = 1e-8
CLAMP = 256.0
GAIN = 1.0 / 16.0
UNROLL = 2
FIRST = 4
LAST = TILES - 4


def build(nc, x, x_turned, sel, idx_pw, idx_kj, pw_table, kj_table, mlp_x, mem_w1, noi_w1, res_w1, mlp_w2, mlp_rows, beta_rows,
          int_w1, int_w2, norm_rows, aw, weight_t, affine_t, affine_b, eye, sel_cmp, out):
    with ExitStack() as ctx:
        def sb(name, shape, dt=F32):
            return ctx.enter_context(nc.sbuf_tensor(name, shape, dt))

        def sem(name):
            return ctx.enter_context(nc.semaphore(name))

        batch_rows_dram = nc.dram_tensor("batch_rows_dram", (BATCH, 2 * D), F32, kind="Internal").ap()

        wname = ("x", "t", "s", "h", "w2", "l1")
        with ExitStack() as before:
            early_hi = {n: before.enter_context(nc.sbuf_tensor(f"early_hi_{n}", [P, C, D], F32))[:] for n in wname}
            raw_w = {n: before.enter_context(nc.sbuf_tensor(f"raw_{n}", [P, C, D], F32))[:] for n in wname}
        w_hi = {n: sb(f"w_hi_{n}", [P, C, D], F32R) for n in wname}
        w_lo = {n: sb(f"w_lo_{n}", [P, C, D], F32R) for n in wname}
        norm_g = sb("norm_g", [P, 4, D])
        ident = sb("ident", [P, P])
        row_table = sb("row_table", [TROWS, D], BF16)
        cmp = sb("cmp", [TROWS, 1])
        pw_ids = sb("pw_ids", [P, TILES], I32)
        kj_ids = sb("kj_ids", [P, 2, TILES], I32)
        kj_index = sb("kj_index", [P, TILES], I32)
        half = sb("half", [P, 1])
        batch_rows = sb("batch_rows", [P, 2, 2 * D])

        work = sb("work", [P, 22 * D])
        place = [0]

        def carve(rows):
            a = place[0]
            place[0] += rows * D
            return work[:, a:a + rows * D].rearrange("p (n d) -> p n d", n=rows)

        gb, gk, z = [None, None], [None, None], [None, None]
        gb[0] = carve(2)
        gk[0] = carve(3)
        z[0] = carve(1)
        gk[1], z[1] = carve(3), carve(1)
        gb[1], xb = carve(2), carve(2)
        hid, vs = carve(1), carve(1)
        place[0] += 2 * D
        x1, yo = carve(2), carve(2)
        assert place[0] == 22 * D
        xt = sb("xt", [P, 2, D])
        xturn = sb("xturn", [P, 2, C, P])
        lhs_hi = {n: sb(f"lhs_hi_{n}", [P, C, P], F32R) for n in wname}
        lhs_lo = {n: sb(f"lhs_lo_{n}", [P, C, P], F32R) for n in wname}
        sel_in = sb("sel_in", [TROWS, 2, P], I32)
        onehot = sb("onehot", [TROWS, 2, P], BF16)
        ids_now = sb("ids_now", [P, 4], I32)
        raw = {n: sb(f"bn_{n}", [P, 2, 6]) for n in "xau"}
        mv = {n: sb(f"mv_{n}", [P, 2, 2]) for n in "xau"}
        ve = {n: sb(f"ve_{n}", [P, 2, 1]) for n in "xau"}
        rs = {n: sb(f"rs_{n}", [P, 2, 1]) for n in "xau"}

        stage = [work[:, (6 + 4 * k) * D:(10 + 4 * k) * D].rearrange("p (c d) -> p c d", c=4) for k in range(4)]
        mlp_w1_in, mlp_w2_in = stage[0], [early_hi[n] for n in ("l1", "w2", "x")]
        wx_part = early_hi["x"]
        wn_in, wr_in, wt_squares = stage[2], stage[3], stage[3]
        aff_raw = stage[0][:, 0:2, :]
        affb = stage[0][0:QUAD, 2, :]
        mrows = stage[1][0:TROWS]
        mx = sb("mx", [P, 4, QUAD])
        mh = sb("mh", [TROWS, D])
        mhT = sb("mhT", [P, C, TROWS])
        rowT = sb("rowT", [P, 6, C, ROWS])
        beta = sb("beta", [QUAD, 4, D])
        style, dcoef = beta[:, 0, :], beta[:, 1, :]
        newton = beta[:, 2, :]
        b1r = beta[0:ROWS, 3, :]
        sqT = mhT[:, :, 0:QUAD]
        soft = sb("soft", [P, 4, 8])
        wsm = soft[:, 3, 0:6]

        pre = ctx.enter_context(nc.psum_tensor("pre", [P, 2, D], F32))
        tb = ctx.enter_context(nc.psum_tensor("tb", [P, 4, D], F32))
        pu = ctx.enter_context(nc.psum_tensor("pu", [P, D], F32))
        py = ctx.enter_context(nc.psum_tensor("py", [P, D], F32))
        table_sum = py[0:ROWS, :]

        ld = {n: sem(f"ld_{n}") for n in (
            "aw", "mx", "mem", "noi", "res", "mlp_b1", "mlp_rest", "beta", "aff", "affb", "m0", "m1", "m2", "ident", "norm",
            "cmp", "ids", "l1", "w_m", "w_n", "w_r", "w_h", "w_t", "w_s", "w_w2")}
        aw_max, aw_exp, aw_ready = sem("aw_max"), sem("aw_exp"), sem("aw_ready")
        mlp1_mm, mlp1_add, mlp_h, h_tr, hT_ready = (sem(n) for n in ("mlp1_mm", "mlp1_add", "mlp_h", "h_tr", "hT_ready"))
        mlp2_mm = sem("mlp2_mm")
        c_var, c_rs, c_ready, c_tr, rowT_c = (sem(n) for n in ("c_var", "c_rs", "c_ready", "c_tr", "rowT_c"))
        styles_mm, styles_ready, styles_sq, sq_tr, sqT_ready = (
            sem(n) for n in ("styles_mm", "styles_ready", "styles_sq", "sq_tr", "sqT_ready"))
        wt_sq, dco_mm, dco_in, dco_root, dco_ready = (sem(n) for n in ("wt_sq", "dco_mm", "dco_in", "dco_root", "dco_ready"))
        style_stored, dcoef_stored = sem("style_stored"), sem("dcoef_stored")
        beta_tr, rowT_b = sem("beta_tr"), sem("rowT_b")
        table_mm = {n: sem(f"table_mm_{n}") for n in "htsmnr"}
        table_ready = sem("table_ready")
        hi_done = {n: sem(f"hi_done_{n}") for n in wname}
        lo_done = {n: sem(f"lo_done_{n}") for n in wname}
        wm_scaled, wn_added, wx_sum = sem("wm_scaled"), sem("wn_added"), sem("wx_sum")
        dve_step = sem("dve_step")
        half_set, kj_ready = sem("half_set"), sem("kj_ready")

        x_loaded = [sem(f"x_loaded_{u}") for u in range(2)]
        sel_loaded = [sem(f"sel_loaded_{u}") for u in range(2)]
        gb_loaded = [sem(f"gb_loaded_{u}") for u in range(2)]
        gk_loaded = [sem(f"gk_loaded_{u}") for u in range(2)]
        out_stored = [sem(f"out_stored_{u}") for u in range(2)]
        xturn_loaded = [sem(f"xturn_loaded_{u}") for u in range(2)]
        style_loaded, dcoef_loaded = sem("style_loaded"), sem("dcoef_loaded")
        ids_copied = sem("ids_copied")
        stats = {n: sem(f"stats_{n}") for n in "xau"}
        meanvar = {n: sem(f"meanvar_{n}") for n in "xau"}
        var_ready = {n: sem(f"var_ready_{n}") for n in "xau"}
        rstd_ready = {n: sem(f"rstd_ready_{n}") for n in "xau"}
        z_ready, zg_ready, a_ready, zh_ready = sem("z_ready"), sem("zg_ready"), sem("a_ready"), sem("zh_ready")
        t_ready, s_ready, h_ready = sem("t_ready"), sem("s_ready"), sem("h_ready")
        xb_ready, onehot_ready = sem("xb_ready"), sem("onehot_ready")
        turned = {n: sem(f"turned_{n}") for n in wname}
        hi_ready = {n: sem(f"hi_ready_{n}") for n in wname}
        lo_ready = {n: sem(f"lo_ready_{n}") for n in wname}
        mm_done = {n: sem(f"mm_done_{n}") for n in wname}
        hid_ready, u_ready, v_ready, x1_ready, x1s_ready = sem("hid_ready"), sem("u_ready"), sem("v_ready"), sem("x1_ready"), sem("x1s_ready")
        ys_ready, yb_ready, yc_ready, out_ready = sem("ys_ready"), sem("yb_ready"), sem("yc_ready"), sem("out_ready")

        def at_least(eng, s, n):
            if not isinstance(n, int) or n > 0:
                eng.wait_ge(s, n)

        def loaded(eng, sems, t, u):
            eng.wait_ge(sems[u], (t - u) * 8 + 16)

        def apart(eng):
            eng.wait_ge(ld["ident"], 16)

        def value(eng, n):
            return n if isinstance(n, int) else eng.to_reg(n)

        def batch_of(t):
            return t // PER_BATCH

        def batch_slot(t, what):
            b = batch_of(t) % 2
            if isinstance(t, int):
                return batch_rows[:, b, what * D:(what + 1) * D]
            return batch_rows[:].rearrange("p b d -> p (b d)")[:, bass.ds(b * (2 * D) + what * D, D)]

        def iterate(eng, body, between=None):
            for i in range(FIRST):
                body(i, i % 2)
                if i == 0 and between:
                    between()
            with eng.Fori(FIRST, LAST, UNROLL) as i:
                for k in range(UNROLL):
                    body(i + k, k)
            for i in range(LAST, TILES + 2):
                body(i, i % 2)

        def has(t):
            return not isinstance(t, int) or 0 <= t < TILES

        def draining(i):
            return isinstance(i, int) and i >= TILES

        def style_in(eng, ops, t, u):
            eng.wait_ge(x1_ready, t + 1)
            eng.wait_ge(style_loaded, batch_of(t) * 16 + 16)
            ops.tensor_tensor(vs[:, 0, :], x1[:, u, :], batch_slot(t, 0), ALU.mult).then_inc(x1s_ready, 1)

        def finish(eng, ops, t, u):
            eng.wait_ge(ys_ready, t + 1)
            ops.tensor_tensor(yo[:, u, :], yo[:, u, :], norm_g[:, 2, :], ALU.add).then_inc(yb_ready, 1)
            apart(eng)
            eng.wait_ge(yb_ready, t + 1)
            ops.tensor_scalar(yo[:, u, :], yo[:, u, :], CLAMP, -CLAMP, ALU.min, ALU.max).then_inc(yc_ready, 1)
            eng.wait_ge(yc_ready, t + 1)
            ops.tensor_tensor(yo[:, u, :], yo[:, u, :], x1[:, u, :], ALU.add).then_inc(out_ready, 1)

        def w1_part(k):
            return int_w1[k * D:(k + 1) * D, :].rearrange("(c p) d -> p c d", p=P)

        block = ctx.enter_context(nc.Block())

        @block.sync
        def _(sp):
            def put(name, place, source):
                sp.dma_start(place, source).then_inc(ld[name], 16)

            def square(w):
                return w.rearrange("(c p) d -> p c d", p=P)

            put("mx", mx[:], mlp_x)
            put("res", mlp_w1_in[0:32, 3, :], res_w1)
            put("noi", mlp_w1_in[0:64, 2, :], noi_w1)
            put("mem", mlp_w1_in[:, 0:2, :], square(mem_w1))
            put("aw", soft[:, 0, 0:6], aw.rearrange("(a k) -> a k", a=1).to_broadcast([P, 6]))
            put("mlp_b1", mrows[:, 0, :], mlp_rows[:, 0, :])
            put("ids", pw_ids[:], idx_pw)
            put("ids", kj_ids[:], idx_kj)
            put("ident", ident[:], eye)
            put("m0", mlp_w2_in[0], square(mlp_w2[0]))
            sp.dma_start(xt[:, 0, :], x[0:P, :]).then_inc(x_loaded[0], 16)
            put("beta", beta[:], beta_rows)
            put("m1", mlp_w2_in[1], square(mlp_w2[1]))
            put("mlp_rest", mrows[:, 1:4, :], mlp_rows[:, 1:4, :])
            put("m2", mlp_w2_in[2], square(mlp_w2[2]))
            put("cmp", cmp[:], sel_cmp)
            sp.dma_start(sel_in[:, 0, :], sel[:, 0:P]).then_inc(sel_loaded[0], 16)
            sp.dma_start(xturn[:, 0, :, :], x_turned[:, 0:P].rearrange("(c p) t -> p c t", p=P)).then_inc(xturn_loaded[0], 16)
            put("w_h", raw_w["h"], w1_part(0))
            sp.wait_ge(mlp1_mm, 1)
            put("aff", aff_raw, affine_t.rearrange("(c p) d -> p c d", p=P))
            put("affb", affb, affine_b)
            put("w_t", raw_w["t"], w1_part(1))
            put("w_m", raw_w["x"], w1_part(2))
            put("w_n", wn_in, w1_part(3))
            put("w_r", wr_in, w1_part(4))
            put("w_s", raw_w["s"], w1_part(5))
            def load(t, u):
                apart(sp)
                at_least(sp, z_ready, t - 1)
                at_least(sp, xb_ready, t - 1)
                sp.dma_start(xt[:, u, :], x[bass.ds(t * P, P), :]).then_inc(x_loaded[u], 16)
                apart(sp)
                at_least(sp, onehot_ready, t - 1)
                sp.dma_start(sel_in[:, u, :], sel[:, bass.ds(t * P, P)]).then_inc(sel_loaded[u], 16)
                apart(sp)
                at_least(sp, lo_ready["x"], t - 1)
                sp.dma_start(xturn[:, u, :, :], x_turned[:, bass.ds(t * P, P)].rearrange("(c p) t -> p c t", p=P)).then_inc(xturn_loaded[u], 16)

            def load_row(b, what, used, arrived):
                apart(sp)
                at_least(sp, used, (b - 1) * PER_BATCH)
                if isinstance(b, int):
                    place = batch_rows[:, b % 2, what * D:(what + 1) * D]
                else:
                    place = batch_rows[:].rearrange("p b d -> p (b d)")[:, bass.ds((b % 2) * (2 * D) + what * D, D)]
                row = batch_rows_dram[bass.ds(b, 1), what * D:(what + 1) * D]
                sp.dma_start(place, row.to_broadcast([P, D])).then_inc(arrived, 16)

            def load_rows(b):
                load_row(b, 0, x1s_ready, style_loaded)
                load_row(b, 1, ys_ready, dcoef_loaded)

            def store(t, u):
                apart(sp)
                sp.wait_ge(out_ready, t + 1)
                sp.dma_start(out[bass.ds(t * P, P), :], yo[:, u, :]).then_inc(out_stored[u], 16)

            load(1, 1)
            put("norm", norm_g[:], norm_rows.rearrange("(a k) d -> a k d", a=1).to_broadcast([P, 4, D]))
            put("l1", raw_w["l1"], square(weight_t))
            put("w_w2", raw_w["w2"], square(int_w2))
            sp.wait_ge(styles_ready, 1)
            sp.dma_start(batch_rows_dram[:, 0:D], style[0:BATCH, :]).then_inc(style_stored, 16)
            sp.wait_ge(style_stored, 16)
            load_row(0, 0, x1s_ready, style_loaded)

            def step(i, u):
                if has(i + 2):
                    load(i + 2, u)
                if has(i - 2):
                    store(i - 2, u)

            for i in range(PER_BATCH):
                if i == 2:
                    sp.wait_ge(dco_ready, 1)
                    sp.dma_start(batch_rows_dram[:, D:2 * D], dcoef[0:BATCH, :]).then_inc(dcoef_stored, 16)
                    sp.wait_ge(dcoef_stored, 16)
                    load_row(0, 1, ys_ready, dcoef_loaded)
                step(i, i % 2)
            with sp.Fori(1, BATCH - 1) as b:
                load_rows(b)
                with sp.Fori(0, PER_BATCH, UNROLL) as k:
                    for u in range(UNROLL):
                        step(b * PER_BATCH + k + u, u)
            load_rows(BATCH - 1)
            for i in range(TILES - PER_BATCH, TILES + 2):
                step(i, i % 2)
            for u in range(2):
                sp.wait_ge(out_stored[u], 8 * TILES)

        @block.gpsimd
        def _(pool):
            nc.gpsimd.memset(half[:], -0.5).then_inc(half_set, 1)
            pool.wait_ge(half_set, 1)
            pool.wait_ge(kj_ready, 1)
            pool.wait_ge(ld["ids"], 32)

            def gather(t, u):
                at_least(pool, h_ready, t - 1)
                at_least(pool, turned["h"], t - 1)
                count = value(pool, 2 * t + 2)
                nc.gpsimd.tensor_copy(ids_now[:, u:u + 1], pw_ids[:, bass.ds(t, 1)]).then_inc(ids_copied, 1)
                nc.gpsimd.tensor_copy(ids_now[:, 2 + u:3 + u], kj_index[:, bass.ds(t, 1)]).then_inc(ids_copied, 1)
                apart(pool)
                pool.wait_ge(ids_copied, count)
                pool.indirect_dma_start(gb[u].rearrange("p n d -> p (n d)"), None, pw_table,
                                        bass.IndirectOffsetOnAxis(ids_now[:, u:u + 1], 0)).then_inc(gb_loaded[u], 16)
                pool.indirect_dma_start(gk[u].rearrange("p n d -> p (n d)"), None, kj_table,
                                        bass.IndirectOffsetOnAxis(ids_now[:, 2 + u:3 + u], 0)).then_inc(gk_loaded[u], 16)

            def rstd(n, t, u):
                pool.wait_ge(var_ready[n], t + 1)
                nc.gpsimd.tensor_tensor(rs[n][:, u, :], ve[n][:, u, :], half[:], ALU.pow).then_inc(rstd_ready[n], 1)

            def ahead(f, v, between=None):
                rstd("x", f, v)
                if between:
                    between()
                pool.wait_ge(z_ready, f + 1)
                loaded(pool, gb_loaded, f, v)
                nc.gpsimd.tensor_tensor(gb[v][:, 0, :], z[v][:, 0, :], gb[v][:, 0, :], ALU.mult).then_inc(zg_ready, 1)
                pool.wait_ge(zg_ready, f + 1)
                nc.gpsimd.tensor_tensor(gb[v][:, 0, :], gb[v][:, 0, :], gb[v][:, 1, :], ALU.add).then_inc(a_ready, 1)
                rstd("a", f, v)

            def add_be(f, v):
                loaded(pool, x_loaded, f, v)
                at_least(pool, x1_ready, f - 1)
                nc.gpsimd.tensor_tensor(xb[:, v, :], xt[:, v, :], norm_g[:, 1, :], ALU.add).then_inc(xb_ready, 1)

            gather(0, 0)

            def rstd_mlps():
                pool.wait_ge(c_var, 1)
                nc.gpsimd.tensor_tensor(rs["u"][0:TROWS, 0, :], ve["u"][0:TROWS, 0, :], half[0:TROWS, :], ALU.pow).then_inc(c_rs, 1)

            ahead(0, 0, rstd_mlps)
            pool.wait_ge(c_ready, 1)
            pool.wait_ge(styles_ready, 1)
            gather(1, 1)
            pool.wait_ge(ld["norm"], 16)
            add_be(0, 0)

            def low_w2():
                pool.wait_ge(hi_done["w2"], 1)
                nc.gpsimd.tensor_tensor(w_lo["w2"][:], raw_w["w2"], w_hi["w2"][:].bitcast(F32), ALU.subtract).then_inc(lo_done["w2"], 1)

            def body(i, u):
                f, v = i + 1, 1 - u
                if has(f):
                    ahead(f, v)
                if has(i + 2):
                    gather(i + 2, u)
                if has(i - 1):
                    rstd("u", i - 1, v)
                if has(i - 2) and not draining(i):
                    finish(pool, nc.gpsimd, i - 2, u)
                if has(i - 1) and not draining(i):
                    style_in(pool, nc.gpsimd, i - 1, v)
                if has(f):
                    add_be(f, v)

            iterate(pool, body, low_w2)

        @block.scalar
        def _(act):
            act.wait_ge(aw_max, 1)
            nc.scalar.activation(soft[:, 1, 0:6], soft[:, 0, 0:6], ACT.Exp, bias=soft[:, 2, 0:1]).then_inc(aw_exp, 1)
            act.wait_ge(mlp1_add, 1)
            nc.scalar.activation(mh[:], mh[:], ACT.Silu).then_inc(mlp_h, 1)

            def high(n, scale=None):
                nc.scalar.activation(w_hi[n][:], raw_w[n], ACT.Copy, scale=1.0 if scale is None else scale).then_inc(hi_done[n], 1)

            def split(n, bank, t):
                act.wait_ge(turned[n], t + 1)
                at_least(act, mm_done[n], t)
                nc.scalar.activation(lhs_hi[n][:].rearrange("p c t -> p (c t)"), tb[:, bank, :], ACT.Copy).then_inc(hi_ready[n], 1)

            def split_x(t, u):
                loaded(act, xturn_loaded, t, u)
                at_least(act, mm_done["x"], t)
                nc.scalar.activation(lhs_hi["x"][:], xturn[:, u, :, :], ACT.Copy).then_inc(hi_ready["x"], 1)

            split_x(0, 0)
            act.wait_ge(aw_ready, 1)
            act.wait_ge(ld["w_h"], 16)
            high("h", wsm[:, 0:1])
            act.wait_ge(ld["w_t"], 16)
            high("t", wsm[:, 1:2])
            act.wait_ge(ld["w_m"], 16)
            act.wait_ge(mlp2_mm, 3)
            nc.scalar.activation(wx_part, raw_w["x"], ACT.Copy, scale=wsm[:, 2:3]).then_inc(wm_scaled, 1)
            split("t", 1, 0)
            act.wait_ge(wx_sum, 1)
            high("x")
            act.wait_ge(ld["w_s"], 16)
            high("s", wsm[:, 5:6])
            act.wait_ge(ld["l1"], 16)
            high("l1")
            act.wait_ge(ld["w_w2"], 16)
            high("w2")
            act.wait_ge(table_mm["r"], 1)
            nc.scalar.activation(wt_squares, raw_w["l1"], ACT.Square).then_inc(wt_sq, 1)

            def root():
                act.wait_ge(dco_in, 1)
                nc.scalar.activation(newton, dcoef, ACT.Sqrt).then_inc(dco_root, 1)

            def body(i, u):
                if has(i - 1):
                    split("w2", 0, i - 1)
                if has(i):
                    split("s", 1, i)
                if has(i - 2):
                    split("l1", 2, i - 2)
                if has(i):
                    split("h", 3, i)
                if has(i + 1):
                    split_x(i + 1, 1 - u)
                    split("t", 1, i + 1)
                if has(i):
                    act.wait_ge(mm_done["h"], i + 1)
                    at_least(act, turned["w2"], i)
                    nc.scalar.activation(hid[:, 0, :], pre[:, u, :], ACT.Silu).then_inc(hid_ready, 1)

            iterate(act, body, root)

        @block.vector
        def _(dve):
            steps = [0]

            def link(ins):
                steps[0] += 1
                ins.then_inc(dve_step, 1)
                dve.wait_ge(dve_step, steps[0])

            dve.wait_ge(ld["aw"], 16)
            link(nc.vector.tensor_reduce(soft[:, 2, 1:2], soft[:, 0, 0:6], AX.X, ALU.max))
            nc.vector.tensor_scalar(soft[:, 2, 0:1], soft[:, 2, 1:2], -1.0, None, ALU.mult).then_inc(aw_max, 1)
            dve.wait_ge(aw_exp, 1)
            link(nc.vector.tensor_reduce(soft[:, 2, 2:3], soft[:, 1, 0:6], AX.X, ALU.add))
            link(nc.vector.reciprocal(soft[:, 2, 3:4], soft[:, 2, 2:3]))
            nc.vector.tensor_scalar(wsm, soft[:, 1, 0:6], soft[:, 2, 3:4], None, ALU.mult).then_inc(aw_ready, 1)
            nc.vector.memset(row_table[:], 0.0)
            link(nc.vector.memset(rowT[:], 0.0))
            dve.wait_ge(mlp1_mm, 1)
            dve.wait_ge(ld["mlp_b1"], 16)
            nc.vector.tensor_tensor(mh[:], tb[0:TROWS, 3, :], mrows[:, 0, :], ALU.add).then_inc(mlp1_add, 1)
            dve.wait_ge(ld["ids"], 32)
            nc.vector.scalar_tensor_tensor(out=kj_index[:], in0=kj_ids[:, 0, :], scalar=float(SCALES), in1=kj_ids[:, 1, :],
                                           op0=ALU.mult, op1=ALU.add).then_inc(kj_ready, 1)
            dve.wait_ge(h_tr, 1)
            nc.vector.tensor_copy(mhT[:].rearrange("p c r -> p (c r)"), tb[:, 0, 0:C * TROWS]).then_inc(hT_ready, 1)

            def moments(n, src, t, u):
                count = value(dve, t + 1)
                nc.vector.bn_stats(raw[n][:, u, :], src).then_inc(stats[n], 1)
                apart(dve)
                dve.wait_ge(stats[n], count)
                nc.vector.bn_aggr(mv[n][:, u, :], raw[n][:, u, :]).then_inc(meanvar[n], 1)
                dve.wait_ge(meanvar[n], t + 1)
                nc.vector.tensor_scalar(ve[n][:, u, :], mv[n][:, u, 1:2], EPS, None, ALU.add).then_inc(var_ready[n], 1)

            def low_part(n, bank, t):
                dve.wait_ge(hi_ready[n], t + 1)
                nc.vector.tensor_tensor(lhs_lo[n][:].rearrange("p c t -> p (c t)"), tb[:, bank, :],
                                        lhs_hi[n][:].rearrange("p c t -> p (c t)").bitcast(F32), ALU.subtract).then_inc(lo_ready[n], 1)

            def low_x(t, u):
                dve.wait_ge(hi_ready["x"], t + 1)
                nc.vector.tensor_tensor(lhs_lo["x"][:], xturn[:, u, :, :], lhs_hi["x"][:].bitcast(F32), ALU.subtract).then_inc(lo_ready["x"], 1)

            def normal(f, v):
                dve.wait_ge(rstd_ready["x"], f + 1)
                at_least(dve, zg_ready, f - 1)
                at_least(dve, s_ready, f - 1)
                nc.vector.tensor_scalar(z[v][:, 0, :], xt[:, v, :], mv["x"][:, v, 0:1], rs["x"][:, v, :],
                                        ALU.subtract, ALU.mult).then_inc(z_ready, 1)

            def gated(f, v):
                dve.wait_ge(z_ready, f + 1)
                loaded(dve, gk_loaded, f, v)
                nc.vector.tensor_tensor(gk[v][:, 1, :], z[v][:, 0, :], gk[v][:, 1, :], ALU.mult).then_inc(t_ready, 1)
                nc.vector.tensor_tensor(gk[v][:, 2, :], z[v][:, 0, :], gk[v][:, 2, :], ALU.mult).then_inc(s_ready, 1)
                loaded(dve, sel_loaded, f, v)
                at_least(dve, mm_done["h"], f - 1)
                nc.vector.tensor_scalar(onehot[:, v, :], sel_in[:, v, :], cmp[:, 0:1], None, ALU.is_equal).then_inc(onehot_ready, 1)

            def second_normal(f, v):
                dve.wait_ge(rstd_ready["a"], f + 1)
                nc.vector.tensor_scalar(gb[v][:, 0, :], gb[v][:, 0, :], mv["a"][:, v, 0:1], rs["a"][:, v, :],
                                        ALU.subtract, ALU.mult).then_inc(zh_ready, 1)
                dve.wait_ge(zh_ready, f + 1)
                nc.vector.tensor_tensor(gk[v][:, 0, :], gb[v][:, 0, :], gk[v][:, 0, :], ALU.mult).then_inc(h_ready, 1)

            loaded(dve, x_loaded, 0, 0)
            moments("x", xt[:, 0, :], 0, 0)
            normal(0, 0)

            dve.wait_ge(beta_tr, 1)
            dve.wait_ge(aw_ready, 1)
            for k, unit in enumerate((0, 1, 5)):
                src = tb[:, 2, k * C * ROWS:(k + 1) * C * ROWS].rearrange("p (c r) -> p c r", c=C)
                nc.vector.tensor_scalar(rowT[:, unit, :, :], src, wsm[:, unit:unit + 1], None, ALU.mult).then_inc(rowT_b, 1)
            dve.wait_ge(mlp2_mm, 3)
            dve.wait_ge(ld["mlp_rest"], 16)
            link(nc.vector.tensor_tensor(mh[:], tb[0:TROWS, 3, :], mrows[:, 1, :], ALU.add))
            link(nc.vector.bn_stats(raw["u"][0:TROWS, 0, :], mh[:]))
            link(nc.vector.bn_aggr(mv["u"][0:TROWS, 0, :], raw["u"][0:TROWS, 0, :]))
            nc.vector.tensor_scalar(ve["u"][0:TROWS, 0, :], mv["u"][0:TROWS, 0, 1:2], EPS, None, ALU.add).then_inc(c_var, 1)
            dve.wait_ge(c_rs, 1)
            link(nc.vector.tensor_scalar(mh[:], mh[:], mv["u"][0:TROWS, 0, 0:1], rs["u"][0:TROWS, 0, :], ALU.subtract, ALU.mult))
            link(nc.vector.tensor_tensor(mh[:], mh[:], mrows[:, 2, :], ALU.mult))
            nc.vector.tensor_tensor(mh[:], mh[:], mrows[:, 3, :], ALU.add).then_inc(c_ready, 1)

            flat = "p c d -> p (c d)"

            def low(n, scale):
                dve.wait_ge(hi_done[n], 1)
                nc.vector.scalar_tensor_tensor(out=w_lo[n][:].rearrange(flat), in0=raw_w[n].rearrange(flat), scalar=scale,
                                               in1=w_hi[n][:].bitcast(F32).rearrange(flat), op0=ALU.mult, op1=ALU.subtract).then_inc(lo_done[n], 1)

            dve.wait_ge(table_mm["h"], 1)
            low("h", wsm[:, 0:1])
            dve.wait_ge(c_tr, 1)
            for m in range(3):
                src = tb[:, 3, 0:C * TROWS].rearrange("p (c r) -> p c r", c=C)[:, :, QUAD * m:QUAD * m + BATCH]
                nc.vector.tensor_scalar(rowT[:, 2 + m, :, 0:BATCH], src, wsm[:, 2 + m:3 + m], None, ALU.mult).then_inc(rowT_c, 1)
            dve.wait_ge(styles_mm, 1)
            dve.wait_ge(ld["affb"], 16)
            nc.vector.scalar_tensor_tensor(out=style, in0=tb[0:QUAD, 2, :], scalar=GAIN, in1=affb,
                                           op0=ALU.mult, op1=ALU.add).then_inc(styles_ready, 1)
            dve.wait_ge(styles_ready, 1)
            nc.vector.tensor_tensor(dcoef, style, style, ALU.mult).then_inc(styles_sq, 1)
            dve.wait_ge(table_mm["t"], 1)
            low("t", wsm[:, 1:2])
            dve.wait_ge(ld["w_n"], 16)
            dve.wait_ge(wm_scaled, 1)
            nc.vector.scalar_tensor_tensor(out=wx_part.rearrange(flat), in0=wn_in.rearrange(flat), scalar=wsm[:, 3:4],
                                           in1=wx_part.rearrange(flat), op0=ALU.mult, op1=ALU.add).then_inc(wn_added, 1)
            dve.wait_ge(ld["cmp"], 16)
            gated(0, 0)
            low_x(0, 0)
            dve.wait_ge(a_ready, 1)
            moments("a", gb[0][:, 0, :], 0, 0)
            second_normal(0, 0)
            dve.wait_ge(sq_tr, 1)
            nc.vector.tensor_copy(sqT, tb[:, 0, 0:C * QUAD].rearrange("p (c r) -> p c r", c=C)).then_inc(sqT_ready, 1)
            dve.wait_ge(ld["w_r"], 16)
            dve.wait_ge(wn_added, 1)
            dve.wait_ge(table_mm["m"], 1)
            nc.vector.scalar_tensor_tensor(out=raw_w["x"].rearrange(flat), in0=wr_in.rearrange(flat), scalar=wsm[:, 4:5],
                                           in1=wx_part.rearrange(flat), op0=ALU.mult, op1=ALU.add).then_inc(wx_sum, 1)
            low_part("t", 1, 0)
            low("x", 1.0)
            dve.wait_ge(table_mm["s"], 1)
            low("s", wsm[:, 5:6])
            link(nc.vector.tensor_tensor(b1r, table_sum, b1r, ALU.add))
            for k in range(PARTS):
                part = row_table[QUAD * k:QUAD * k + ROWS, :]
                if k + 1 == PARTS:
                    nc.vector.tensor_copy(part, b1r).then_inc(table_ready, 1)
                else:
                    link(nc.vector.tensor_copy(part, b1r))
                    link(nc.vector.tensor_copy(mh[0:ROWS, :], part))
                    link(nc.vector.tensor_tensor(b1r, b1r, mh[0:ROWS, :], ALU.subtract))
            dve.wait_ge(ld["norm"], 16)

            def low_l1():
                dve.wait_ge(wt_sq, 1)
                low("l1", 1.0)

            def demod_in():
                low_l1()
                dve.wait_ge(dco_mm, 1)
                nc.vector.tensor_scalar(dcoef, py[0:QUAD, :], DEMOD_EPS, None, ALU.add).then_inc(dco_in, 1)

            def demod_out():
                dve.wait_ge(dco_root, 1)
                r, q = newton, mh[0:QUAD, :]
                link(nc.vector.reciprocal(r, r))
                link(nc.vector.tensor_tensor(q, r, r, ALU.mult))
                link(nc.vector.tensor_tensor(q, q, dcoef, ALU.mult))
                link(nc.vector.tensor_scalar(q, q, -0.5, 1.5, ALU.mult, ALU.add))
                nc.vector.tensor_tensor(dcoef, q, r, ALU.mult).then_inc(dco_ready, 1)

            def body(i, u):
                f, v = i + 1, 1 - u
                if has(f):
                    loaded(dve, x_loaded, f, v)
                    moments("x", xt[:, v, :], f, v)
                if has(i - 1):
                    low_part("w2", 0, i - 1)
                if has(f):
                    normal(f, v)
                if has(i):
                    low_part("s", 1, i)
                if has(f):
                    gated(f, v)
                if has(i - 2):
                    low_part("l1", 2, i - 2)
                if has(i):
                    low_part("h", 3, i)
                if has(f):
                    dve.wait_ge(a_ready, f + 1)
                    moments("a", gb[v][:, 0, :], f, v)
                if has(i - 1):
                    t = i - 1
                    dve.wait_ge(mm_done["w2"], t + 1)
                    at_least(dve, turned["l1"], t)
                    nc.vector.tensor_tensor(vs[:, 0, :], pu[:], norm_g[:, 3, :], ALU.add).then_inc(u_ready, 1)
                    dve.wait_ge(u_ready, t + 1)
                    moments("u", vs[:, 0, :], t, v)
                if has(f):
                    second_normal(f, v)
                if has(i - 1):
                    nc.vector.scalar_tensor_tensor(out=vs[:, 0, :], in0=vs[:, 0, :], scalar=mv["u"][:, v, 0:1], in1=norm_g[:, 0, :],
                                                   op0=ALU.subtract, op1=ALU.mult).then_inc(v_ready, 1)
                    dve.wait_ge(rstd_ready["u"], t + 1)
                    dve.wait_ge(v_ready, t + 1)
                    dve.wait_ge(xb_ready, t + 1)
                    at_least(dve, out_ready, t - 1)
                    nc.vector.scalar_tensor_tensor(out=x1[:, v, :], in0=vs[:, 0, :], scalar=rs["u"][:, v, :], in1=xb[:, v, :],
                                                   op0=ALU.mult, op1=ALU.add).then_inc(x1_ready, 1)
                    if draining(i):
                        style_in(dve, nc.vector, t, v)
                if has(i - 2):
                    t = i - 2
                    dve.wait_ge(mm_done["l1"], t + 1)
                    dve.wait_ge(dcoef_loaded, batch_of(t) * 16 + 16)
                    if not isinstance(t, int) or t >= 2:
                        loaded(dve, out_stored, t - 2, u)
                    nc.vector.tensor_tensor(yo[:, u, :], py[:], batch_slot(t, 1), ALU.mult).then_inc(ys_ready, 1)
                    if draining(i):
                        finish(dve, nc.vector, t, u)
                if has(f):
                    low_x(f, v)
                    low_part("t", 1, f)
                if isinstance(i, int) and i == 1:
                    demod_out()

            iterate(dve, body, demod_in)

        @block.tensor
        def _(pe):
            pe.wait_ge(ld["mx"], 16)
            for m, n, chunks, rows in ((2, "res", (3,), 32), (1, "noi", (2,), 64), (0, "mem", (0, 1), P)):
                pe.wait_ge(ld[n], 16)
                for c in chunks:
                    last = pe.matmul(tb[QUAD * m:QUAD * (m + 1), 3, :], mx[0:rows, c, :], mlp_w1_in[0:rows, c, :],
                                     start=c == chunks[0], stop=c == chunks[-1])
            last.then_inc(mlp1_mm, 1)
            pe.wait_ge(ld["ident"], 16)
            pe.wait_ge(mlp_h, 1)
            for c in range(C):
                last = pe.transpose(tb[:, 0, c * TROWS:(c + 1) * TROWS], mh[:, c * P:(c + 1) * P], ident[0:TROWS, 0:TROWS])
            last.then_inc(h_tr, 1)

            def turn(n, bank, src):
                for c in range(C):
                    last = pe.transpose(tb[:, bank, c * P:(c + 1) * P], src[:, c * P:(c + 1) * P], ident[:])
                last.then_inc(turned[n], 1)

            pe.wait_ge(hT_ready, 1)
            for m in range(3):
                pe.wait_ge(ld[f"m{m}"], 16)
                quad = slice(QUAD * m, QUAD * (m + 1))
                for c in range(C):
                    last = pe.matmul(tb[quad, 3, :], mhT[:, c, quad], mlp_w2_in[m][:, c, :], start=c == 0, stop=c == C - 1)
                last.then_inc(mlp2_mm, 1)

            pe.wait_ge(ld["beta"], 16)
            for k in range(3):
                for c in range(C):
                    at = (k * C + c) * ROWS
                    last = pe.transpose(tb[:, 2, at:at + ROWS], beta[0:ROWS, k, c * P:(c + 1) * P], ident[0:ROWS, 0:ROWS])
            last.then_inc(beta_tr, 1)

            def table(n, unit, w, first=False, last_one=False):
                pe.wait_ge(ld[f"w_{n}"], 16)
                for c in range(C):
                    last = pe.matmul(table_sum, rowT[:, unit, c, :], w[:, c, :],
                                     start=first and c == 0, stop=last_one and c == C - 1)
                last.then_inc(table_mm[n], 1)

            pe.wait_ge(rowT_b, 3)
            table("h", 0, raw_w["h"], first=True)
            pe.wait_ge(c_ready, 1)
            for c in range(C):
                last = pe.transpose(tb[:, 3, c * TROWS:(c + 1) * TROWS], mh[:, c * P:(c + 1) * P], ident[0:TROWS, 0:TROWS])
            last.then_inc(c_tr, 1)
            pe.wait_ge(ld["aff"], 16)
            for c in range(2):
                last = pe.matmul(tb[0:QUAD, 2, :], mx[:, c, :], aff_raw[:, c, :], start=c == 0, stop=c == 1)
            last.then_inc(styles_mm, 1)
            table("t", 1, raw_w["t"])
            pe.wait_ge(rowT_c, 3)
            table("m", 2, raw_w["x"])
            table("n", 3, wn_in)
            pe.wait_ge(styles_sq, 1)
            for c in range(C):
                last = pe.transpose(tb[:, 0, c * QUAD:(c + 1) * QUAD], dcoef[:, c * P:(c + 1) * P], ident[0:QUAD, 0:QUAD])
            last.then_inc(sq_tr, 1)
            pe.wait_ge(t_ready, 1)
            turn("t", 1, gk[0][:, 1, :])
            table("r", 4, wr_in)
            table("s", 5, raw_w["s"], last_one=True)

            def demod():
                pe.wait_ge(sqT_ready, 1)
                pe.wait_ge(wt_sq, 1)
                for c in range(C):
                    last = pe.matmul(py[0:QUAD, :], sqT[:, c, :], wt_squares[:, c, :], start=c == 0, stop=c == C - 1)
                last.then_inc(dco_mm, 1)

            def unit(n, t, dst, start, stop):
                if isinstance(t, int) and t == 0:
                    pe.wait_ge(lo_done[n], 1)
                passes = ((lhs_hi, w_hi), (lhs_hi, w_lo), (lhs_lo, w_hi))
                for c in range(C):
                    for k, (a, b) in enumerate(passes):
                        last = pe.matmul(dst, a[n][:, c, :], b[n][:, c, :], start=start and c == 0 and k == 0,
                                         stop=stop and c == C - 1 and k == 2)
                last.then_inc(mm_done[n], 1)

            def body(i, u):
                v = 1 - u
                if has(i):
                    at_least(pe, hid_ready, i - 1)
                    pe.wait_ge(lo_ready["x"], i + 1)
                    unit("x", i, pre[:, u, :], True, False)
                if has(i - 1):
                    pe.wait_ge(hid_ready, i)
                    turn("w2", 0, hid[:, 0, :])
                if has(i):
                    pe.wait_ge(s_ready, i + 1)
                    pe.wait_ge(lo_ready["t"], i + 1)
                    turn("s", 1, gk[u][:, 2, :])
                    unit("t", i, pre[:, u, :], False, False)
                if has(i - 2):
                    pe.wait_ge(x1s_ready, i - 1)
                    at_least(pe, lo_ready["l1"], i - 2)
                    turn("l1", 2, vs[:, 0, :])
                if has(i):
                    pe.wait_ge(h_ready, i + 1)
                    at_least(pe, lo_ready["h"], i)
                    turn("h", 3, gk[u][:, 0, :])
                if has(i - 1):
                    pe.wait_ge(lo_ready["w2"], i)
                    at_least(pe, u_ready, i - 1)
                    unit("w2", i - 1, pu[:], True, True)
                if has(i - 2):
                    pe.wait_ge(lo_ready["l1"], i - 1)
                    if isinstance(i, int) and i == 2:
                        pe.wait_ge(dco_in, 1)
                    at_least(pe, ys_ready, i - 2)
                    unit("l1", i - 2, py[:], True, True)
                if has(i):
                    pe.wait_ge(lo_ready["s"], i + 1)
                    unit("s", i, pre[:, u, :], False, False)
                if has(i + 1):
                    pe.wait_ge(t_ready, i + 2)
                    turn("t", 1, gk[v][:, 1, :])
                if has(i):
                    pe.wait_ge(onehot_ready, i + 1)
                    if isinstance(i, int) and i == 0:
                        pe.wait_ge(table_ready, 1)
                    pe.matmul(pre[:, u, :], onehot[:, u, :], row_table[:], start=False, stop=False)
                    pe.wait_ge(lo_ready["h"], i + 1)
                    unit("h", i, pre[:, u, :], False, True)

            iterate(pe, body, demod)


def kernel(**inputs):
    import numpy as np
    import concourse.bacc as bacc
    from concourse.bass_utils import run_bass_kernel_spmd

    a = {k: np.asarray(v) for k, v in inputs.items()}
    g = {k[len("L0_cond_"):]: v for k, v in a.items() if k.startswith("L0_cond_")}
    f32 = np.float32

    def by_tile(ids):
        return ids.reshape(TILES, P).T

    kinds, scales = a["itok_BxS_0_4"], a["mask_BxS_ik0"]
    sel = np.full((TROWS, BATCH * SEQ), -1, np.int32)
    cmp = np.zeros((TROWS, 1), f32)
    for k in range(PARTS):
        r = QUAD * k
        sel[r:r + BATCH] = np.repeat(np.arange(BATCH, dtype=np.int32), SEQ)
        sel[r + BATCH:r + BATCH + KINDS] = kinds.reshape(-1)
        sel[r + BATCH + KINDS:r + ROWS] = scales.reshape(-1)
        cmp[r:r + ROWS, 0] = [*range(BATCH), *range(KINDS), *range(SCALES)]
    mlp_x = np.zeros((P, 4, QUAD), f32)
    mlp_x[:, 0:2, 0:BATCH] = a["cond_512"].T.reshape(2, P, BATCH).transpose(1, 0, 2)
    mlp_x[0:64, 2, 0:BATCH] = a["cond_64"].T
    mlp_x[0:32, 3, 0:BATCH] = a["fside_Bx32_0"].T
    mlp_rows = np.zeros((TROWS, 4, D), f32)
    for m, n in enumerate(("mem", "noi", "res")):
        for k, row in enumerate(("b1", "b2", "g", "be")):
            mlp_rows[QUAD * m:QUAD * (m + 1), k] = g[f"{n}_{row}"]
    beta = np.zeros((QUAD, 4, D), f32)
    beta[BATCH:BATCH + KINDS, 0] = g["cp_b"]
    beta[BATCH:BATCH + KINDS, 1] = g["tm_b"]
    beta[BATCH + KINDS:ROWS, 2] = g["ms_b"]
    beta[0:BATCH, 3] = g["int_b1"]
    arrays = {
        "x_in": a["x"].reshape(BATCH * SEQ, D),
        "x_turned": a["x"].reshape(BATCH * SEQ, D).T,
        "sel_ids": sel,
        "idx_pw": by_tile(a["itok_BxS_0_999"]),
        "idx_kj": np.stack([by_tile(kinds), by_tile(scales)], 1),
        "pw_table": np.concatenate([g["pw_g"], g["pw_b"]], 1),
        "kj_table": np.concatenate([np.repeat(g["cp_g"], SCALES, 0), np.repeat(g["tm_g"], SCALES, 0),
                                    np.tile(g["ms_g"], (KINDS, 1))], 1),
        "mlp_x": mlp_x, "mem_w1": g["mem_W1"], "noi_w1": g["noi_W1"], "res_w1": g["res_W1"],
        "mlp_w2": np.stack([g["mem_W2"], g["noi_W2"], g["res_W2"]]),
        "mlp_rows": mlp_rows, "beta_rows": beta,
        "int_w1": g["int_W1"], "int_w2": g["int_W2"],
        "norm_rows": np.stack([g["int_g"], g["int_be"], a["L1_cond_bias"], g["int_b2"]]),
        "aw": g["aw"],
        "weight_t": a["L1_cond_weight"].T, "affine_t": a["L1_cond_affine_w"].T,
        "affine_b": np.broadcast_to(a["L1_cond_affine_b"], (QUAD, D)),
        "eye": np.eye(P, dtype=f32), "sel_cmp": cmp,
    }
    arrays = {k: np.ascontiguousarray(v) for k, v in arrays.items()}
    nc = bacc.Bacc("TRN2", target_bir_lowering=False, num_devices=1)
    args = [nc.dram_tensor(k, v.shape, mybir.dt.from_np(v.dtype), kind="ExternalInput").ap() for k, v in arrays.items()]
    args.append(nc.dram_tensor("out", (BATCH * SEQ, D), F32, kind="ExternalOutput").ap())
    build(nc, *args)
    result = run_bass_kernel_spmd(nc, [arrays], core_ids=[0])
    return result.results[0]["out"].reshape(BATCH, SEQ, D)
```
